# Optimizing a Trainium2 kernel written in Bass

```python
import numpy as np
import jax
import jax.numpy as jnp

def _softmax(x, axis=-1):
    return jax.nn.softmax(x, axis=axis)

def _gelu(x):
    return jax.nn.gelu(x, approximate=True)

def _silu(x):
    return jax.nn.silu(x)

def _sigmoid(x):
    return jax.nn.sigmoid(x)

def _layernorm(x, axis=-1, eps=1e-05):
    m = jnp.mean(x, axis=axis, keepdims=True)
    v = jnp.var(x, axis=axis, keepdims=True)
    return (x - m) / jnp.sqrt(v + eps)

def _scatter_add(tgt, idx, src, axis=0):
    return tgt.at[idx].add(src)

def _segment_sum(src, seg, n):
    return jax.ops.segment_sum(src, seg, n)
kernel_name = 'mk_seq_preln_d1_jaxref_r8_59a9e0'

def setup_inputs(seed: int=0):
    np.random.seed(seed)
    _w = jnp.asarray

    def _L0_attn_setup():
        import jax, jax.numpy as jnp
        import numpy as np
        B, S, D = (4, 512, 128)
        H = 8
        DK = D // H
        DV = D // H
        KLEPE = 5
        ROPE_BASE = 10000.0

        def rotate_half(x):
            x1, x2 = jnp.split(x, 2, axis=-1)
            return jnp.concatenate([-x2, x1], axis=-1)

        def rope_sin_cos(seq_len, dim):
            inv_freq = 1.0 / ROPE_BASE ** (jnp.arange(0, dim, 2, dtype=jnp.float32) / dim)
            freqs = jnp.arange(seq_len, dtype=jnp.float32)[:, None] * inv_freq[None, :]
            emb = jnp.concatenate([freqs, freqs], axis=-1)
            return (jnp.sin(emb), jnp.cos(emb))

        def mala_attn(q, k, v):
            sin, cos = rope_sin_cos(q.shape[1], q.shape[-1])
            sin, cos = (sin[None, :, None, :], cos[None, :, None, :])
            q = q * cos + rotate_half(q) * sin
            k = k * cos + rotate_half(k) * sin
            scale = q.shape[-1] ** (-0.5)
            seq_len = q.shape[1]
            kv = jnp.einsum('bshd,bshe->bhde', k, v)
            ksum = k.sum(axis=1)
            vsum = v.sum(axis=1)
            num = jnp.einsum('bshd,bhde->bshe', q, kv) * scale + vsum[:, None, :, :]
            den = jnp.einsum('bshd,bhd->bsh', q, ksum) * scale + seq_len
            return num / den[..., None]

        def lepe_conv(v, w, b):
            Bb, Ss = (v.shape[0], v.shape[1])
            x = v.transpose(0, 2, 3, 1).reshape(Bb, H * DV, Ss)
            y = jax.lax.conv_general_dilated(x, w, window_strides=(1,), padding=[(KLEPE // 2, KLEPE // 2)], dimension_numbers=('NCH', 'OIH', 'NCH'), feature_group_count=H * DV)
            y = y + b[None, :, None]
            return y.reshape(Bb, H, DV, Ss).transpose(0, 3, 1, 2)
        key = jax.random.key(seed)
        ks = jax.random.split(key, 8)
        w = 0.02
        return {'hidden_states': jax.random.normal(ks[0], (B, S, D), dtype=jnp.float32), 'Wq': jax.random.normal(ks[1], (D, D), dtype=jnp.float32) * w, 'Wk': jax.random.normal(ks[2], (D, D), dtype=jnp.float32) * w, 'Wv': jax.random.normal(ks[3], (D, D), dtype=jnp.float32) * w, 'Wg': jax.random.normal(ks[4], (D, D), dtype=jnp.float32) * w, 'Wo': jax.random.normal(ks[5], (D, D), dtype=jnp.float32) * w, 'lepe_w': jax.random.normal(ks[6], (D, 1, KLEPE), dtype=jnp.float32) * 0.1, 'lepe_b': jnp.zeros((D,), dtype=jnp.float32)}
    _L0_attn_in = _L0_attn_setup()

    def _L0_ffn_setup():
        import jax, jax.numpy as jnp
        import numpy as np
        TOP_K = 2
        key = jax.random.key(seed)
        ks = jax.random.split(key, 6)
        B, S, H, F, E = (4, 256, 128, 512, 8)
        scale = 0.02
        x = jax.random.normal(ks[0], (B, S, H), dtype=jnp.float32)
        gate_w = jax.random.normal(ks[1], (E, H), dtype=jnp.float32) * scale
        w1 = jax.random.normal(ks[2], (E, H, F), dtype=jnp.float32) * scale
        b1 = jnp.zeros((E, F), dtype=jnp.float32)
        w2 = jax.random.normal(ks[3], (E, F, H), dtype=jnp.float32) * scale
        b2 = jnp.zeros((E, H), dtype=jnp.float32)
        return {'x': x, 'gate_w': gate_w, 'w1': w1, 'b1': b1, 'w2': w2, 'b2': b2}
    _L0_ffn_in = _L0_ffn_setup()
    _d = {'L0_attn_hidden_states': _L0_attn_in['hidden_states'], 'L0_attn_Wq': _L0_attn_in['Wq'], 'L0_attn_Wk': _L0_attn_in['Wk'], 'L0_attn_Wv': _L0_attn_in['Wv'], 'L0_attn_Wg': _L0_attn_in['Wg'], 'L0_attn_Wo': _L0_attn_in['Wo'], 'L0_attn_lepe_w': _L0_attn_in['lepe_w'], 'L0_attn_lepe_b': _L0_attn_in['lepe_b'], 'L0_ffn_gate_w': _L0_ffn_in['gate_w'], 'L0_ffn_w1': _L0_ffn_in['w1'], 'L0_ffn_b1': _L0_ffn_in['b1'], 'L0_ffn_w2': _L0_ffn_in['w2'], 'L0_ffn_b2': _L0_ffn_in['b2']}
    _x0 = _d['L0_attn_hidden_states']
    _d['L0_attn_hidden_states'] = jax.random.normal(jax.random.fold_in(jax.random.key(seed), 1), (16, 512, 128), dtype=_x0.dtype)
    del _x0
    return _d

def reference(L0_attn_hidden_states, L0_attn_Wq, L0_attn_Wk, L0_attn_Wv, L0_attn_Wg, L0_attn_Wo, L0_attn_lepe_w, L0_attn_lepe_b, L0_ffn_gate_w, L0_ffn_w1, L0_ffn_b1, L0_ffn_w2, L0_ffn_b2):

    def _L0_attn_ref(hidden_states, Wq, Wk, Wv, Wg, Wo, lepe_w, lepe_b):
        import jax, jax.numpy as jnp
        import numpy as np
        B, S, D = (4, 512, 128)
        H = 8
        DK = D // H
        DV = D // H
        KLEPE = 5
        ROPE_BASE = 10000.0

        def rotate_half(x):
            x1, x2 = jnp.split(x, 2, axis=-1)
            return jnp.concatenate([-x2, x1], axis=-1)

        def rope_sin_cos(seq_len, dim):
            inv_freq = 1.0 / ROPE_BASE ** (jnp.arange(0, dim, 2, dtype=jnp.float32) / dim)
            freqs = jnp.arange(seq_len, dtype=jnp.float32)[:, None] * inv_freq[None, :]
            emb = jnp.concatenate([freqs, freqs], axis=-1)
            return (jnp.sin(emb), jnp.cos(emb))

        def mala_attn(q, k, v):
            sin, cos = rope_sin_cos(q.shape[1], q.shape[-1])
            sin, cos = (sin[None, :, None, :], cos[None, :, None, :])
            q = q * cos + rotate_half(q) * sin
            k = k * cos + rotate_half(k) * sin
            scale = q.shape[-1] ** (-0.5)
            seq_len = q.shape[1]
            kv = jnp.einsum('bshd,bshe->bhde', k, v)
            ksum = k.sum(axis=1)
            vsum = v.sum(axis=1)
            num = jnp.einsum('bshd,bhde->bshe', q, kv) * scale + vsum[:, None, :, :]
            den = jnp.einsum('bshd,bhd->bsh', q, ksum) * scale + seq_len
            return num / den[..., None]

        def lepe_conv(v, w, b):
            Bb, Ss = (v.shape[0], v.shape[1])
            x = v.transpose(0, 2, 3, 1).reshape(Bb, H * DV, Ss)
            y = jax.lax.conv_general_dilated(x, w, window_strides=(1,), padding=[(KLEPE // 2, KLEPE // 2)], dimension_numbers=('NCH', 'OIH', 'NCH'), feature_group_count=H * DV)
            y = y + b[None, :, None]
            return y.reshape(Bb, H, DV, Ss).transpose(0, 3, 1, 2)
        Bb, Ss, _ = hidden_states.shape
        q = (hidden_states @ Wq.T).reshape(Bb, Ss, H, DK)
        k = (hidden_states @ Wk.T).reshape(Bb, Ss, H, DK)
        v = (hidden_states @ Wv.T).reshape(Bb, Ss, H, DV)
        o_gate = hidden_states @ Wg.T
        o = mala_attn(q, k, v) + lepe_conv(v, lepe_w, lepe_b)
        o = o.reshape(Bb, Ss, H * DV) * o_gate
        return o @ Wo.T

    def _L0_ffn_ref(x, gate_w, w1, b1, w2, b2):
        import jax, jax.numpy as jnp
        import numpy as np
        TOP_K = 2
        E = gate_w.shape[0]
        gate_logits = jnp.einsum('bsh,eh->bse', x, gate_w)
        gate_probs = jax.nn.softmax(gate_logits, axis=-1)
        top_v, top_i = jax.lax.top_k(gate_probs, TOP_K)
        onehot = jax.nn.one_hot(top_i, E, dtype=x.dtype)
        comb_w = jnp.einsum('bsk,bske->bse', top_v, onehot)
        out = jnp.zeros_like(x)
        for e in range(E):
            h = jax.nn.silu(jnp.einsum('bsh,hf->bsf', x, w1[e]) + b1[e])
            y = jnp.einsum('bsf,fh->bsh', h, w2[e]) + b2[e]
            out = out + y * comb_w[..., e:e + 1]
        return out
    x = L0_attn_hidden_states
    x = x + _L0_attn_ref(_layernorm(x, axis=-1), L0_attn_Wq, L0_attn_Wk, L0_attn_Wv, L0_attn_Wg, L0_attn_Wo, L0_attn_lepe_w, L0_attn_lepe_b)
    x = x + _L0_ffn_ref(_layernorm(x, axis=-1), L0_ffn_gate_w, L0_ffn_w1, L0_ffn_b1, L0_ffn_w2, L0_ffn_b2)
    return x

_drawn_inputs = setup_inputs


def setup_inputs(seed=0):
    import zlib

    import numpy as np

    out = dict(_drawn_inputs(seed))
    spreads = {'L0_attn_lepe_b': (0.0, 0.8), 'L0_ffn_b1': (0.0, 2.0), 'L0_ffn_b2': (0.0, 2.0)}
    factors = {'L0_attn_Wq': 8.0,
     'L0_attn_Wk': 8.0,
     'L0_attn_Wv': 8.0,
     'L0_attn_Wg': 8.0,
     'L0_attn_Wo': 8.0,
     'L0_attn_lepe_w': 8.0,
     'L0_ffn_w1': 4.716,
     'L0_ffn_w2': 4.326}
    for name, (base, spread) in spreads.items():
        noise = np.random.default_rng([zlib.crc32(name.encode()), seed]).standard_normal(out[name].shape)
        drawn = base * np.exp(spread * noise) if base else spread * noise
        out[name] = jnp.asarray(drawn.astype(out[name].dtype))
    for name, factor in factors.items():
        out[name] = (out[name] * factor).astype(out[name].dtype)
    return out
```

```python
from contextlib import ExitStack

import numpy as np
import concourse.bass as bass
from concourse import mybir

ALU = mybir.AluOpType
ACT = mybir.ActivationFunctionType
F32 = mybir.dt.float32
AX_X = mybir.AxisListType.X

P = 128
NB = 16
S = 512
SUB = S // P
D = 128
H = 8
DK = D // H
TAPS = 5
PAD = TAPS // 2
E = 8
F = 512
FC = F // P
EPS = 1e-5
ND = D + H


def build(nc, x, w_proj, w_o, cos_t, sin_t, head_mask, ident, lepe_w, lepe_b, gate_t, rank_w, w1, b1, w2, b2, out):
    with ExitStack() as ctx:
        def sb(name, shape, dt=F32):
            return ctx.enter_context(nc.sbuf_tensor(name, shape, dt))

        def bank(name):
            return ctx.enter_context(nc.psum_tensor(name, [P, 512], F32))

        def sem(name):
            return ctx.enter_context(nc.semaphore(name))

        wproj = sb("wproj", [P, 6, D])
        wo = sb("wo", [P, D])
        cosT = sb("cosT", [P, S])
        sinT = sb("sinT", [P, S])
        hmask = sb("hmask", [P, ND])
        idn = sb("idn", [P, P])
        lw = sb("lw", [P, TAPS])
        lb = sb("lb", [P, 1])
        gateT = sb("gateT", [P, E])
        rankw = sb("rankw", [P, SUB, E])
        w1s = sb("w1s", [P, E, F])
        w2s = sb("w2s", [P, E, FC, D])
        b1s = sb("b1s", [P, E, FC])
        b2s = sb("b2s", [E, D])
        half = sb("half", [P, SUB])
        ones_row = sb("ones_row", [1, P])

        xres = sb("xres", [P, NB * SUB, D])
        yT_all = sb("yT_all", [P, NB, S])
        comb_all = sb("comb_all", [P, NB * SUB, E])

        st1 = sb("st1", [P, SUB, 6])
        mv1 = sb("mv1", [P, SUB, 2])
        ve1 = sb("ve1", [P, SUB])
        rs1 = sb("rs1", [P, SUB])
        st2 = sb("st2", [P, SUB, 6])
        mv2 = sb("mv2", [P, SUB, 2])
        ve2 = sb("ve2", [P, SUB])
        rs2 = sb("rs2", [P, SUB])
        xin = [sb(f"xin{i}", [P, SUB, D]) for i in range(2)]
        x2 = sb("x2", [P, SUB, D])
        xn = sb("xn", [P, SUB, D])
        xnT = sb("xnT", [P, S])
        q_c = sb("q_c", [P, S])
        q_s = sb("q_s", [P, S])
        k_c = sb("k_c", [P, S])
        k_s = sb("k_s", [P, S])
        qrot = [sb(f"qrot{i}", [P, S]) for i in range(2)]
        krot = [sb(f"krot{i}", [P, S]) for i in range(2)]
        vpad = [sb(f"vpad{i}", [P, S + 2 * PAD]) for i in range(2)]
        vsum = [sb(f"vsum{i}", [P, 1]) for i in range(2)]
        gT = [sb(f"gT{i}", [P, S]) for i in range(2)]
        ktok = sb("ktok", [P, SUB, D])
        vtok = sb("vtok", [P, SUB, D + 1])
        vrow = sb("vrow", [1, ND])
        kvbd = sb("kvbd", [P, ND])
        rden = sb("rden", [P, SUB, H])
        att = sb("att", [P, SUB, D])
        lep = sb("lep", [P, S])
        oT = sb("oT", [P, S])
        yn = sb("yn", [P, SUB, D])
        yT = sb("yT", [P, S])
        lg = sb("lg", [P, SUB, E])
        ex = sb("ex", [P, SUB, E])
        pr = sb("pr", [P, SUB, E])
        oh1 = sb("oh1", [P, SUB, E])
        oh2 = sb("oh2", [P, SUB, E])
        tmp8 = sb("tmp8", [P, SUB, E])
        red = sb("red", [P, SUB])

        combS = sb("combS", [P, SUB, E])
        combT = sb("combT", [E, S])
        hS = [sb(f"hS{i}", [P, S]) for i in range(4)]
        accS = sb("accS", [P, SUB, D])

        P0, P1, P2, T1, KV, N0, N1, B1 = [bank(f"bank{i}") for i in range(8)]
        NN = [N0, N1]

        names = """consts_in x_in xin_full0 xin_full1 x2_kept consts_set ones_set
            ln1_stats ln1_mv ln1_ve ln1_rs xn_ready xnT_psum xnT_ready
            q_psum qp_psum k_psum kp_psum v_psum g_psum
            q_cos q_sin k_cos k_sin q_rot k_rot v_saved g_saved
            k_tr v_tr vs_tr k_tok v_tok v_row kv_psum kv_masked ks_masked
            num0 num1 rden_ready att_ready a_tr lep_chain o_ready
            wo_psum x2_ready ln2_stats ln2_mv ln2_ve ln2_rs yn_ready y_tr yT_ready yT_kept gate_psum
            lg_sub ex_ready rt comb_ready
            cs_ready ct_psum ct_ready b2_psum acc_ready h_psum h_ready y_psum acc_step out_done""".split()
        s = {n: sem(n) for n in names}

        def after(eng, name, n, alone=False):
            if isinstance(n, int) and n <= 0:
                return
            eng.wait_ge(s[name], n)
            if alone:
                eng.nop(nofuse=True)

        block = ctx.enter_context(nc.Block())

        def pipeline(eng, step):
            for i in range(4):
                step(i, i % 2)
            with eng.Fori(4, NB - 2, 2) as i:
                step(i, 0)
                step(i + 1, 1)
            for i in range(NB - 2, NB + 3):
                step(i, i % 2)

        def on(i, lag):
            return not isinstance(i, int) or 0 <= i - lag < NB

        @block.sync
        def _(sp):
            for dst, src in ((idn, ident), (wproj, w_proj), (cosT, cos_t), (sinT, sin_t), (hmask, head_mask), (wo, w_o),
                             (lw, lepe_w), (lb, lepe_b), (gateT, gate_t), (rankw, rank_w)):
                sp.dma_start(dst[:], src).then_inc(s["consts_in"], 16)
            sp.dma_start(b1s[:], b1).then_inc(s["consts_in"], 16)
            sp.dma_start(b2s[:], b2).then_inc(s["consts_in"], 16)
            sp.dma_start(w1s[:], w1.rearrange("e d f -> d e f")).then_inc(s["consts_in"], 16)
            sp.dma_start(w2s[:], w2.rearrange("e (c p) d -> p e c d", p=P)).then_inc(s["consts_in"], 16)
            xv = x.rearrange("(b j p) d -> p (b j) d", p=P, j=SUB)
            for b in range(2):
                sp.dma_start(xin[b][:], xv[:, b * SUB:(b + 1) * SUB, :]).then_inc(s[f"xin_full{b}"], 16)
            with sp.Fori(2, NB - 1, 2) as b:
                for o in range(2):
                    after(sp, "xn_ready", b + o - 1)
                    sp.dma_start(xin[o][:], xv[:, bass.ds((b + o) * SUB, SUB), :]).then_inc(s[f"xin_full{o}"], 16)
            with sp.Fori(0, NB) as b:
                after(sp, "acc_step", (b + 1) * (E * SUB))
                sp.dma_start(out.rearrange("(b j p) d -> p (b j) d", p=P, j=SUB)[:, bass.ds(b * SUB, SUB), :],
                             xres[:, bass.ds(b * SUB, SUB), :]).then_inc(s["out_done"], 16)
            sp.wait_ge(s["out_done"], 16 * NB)

        N_CONST = 14 * 16

        @block.tensor
        def _(pe):
            def transposes(dst, src, name):
                for j in range(SUB):
                    last = nc.tensor.transpose(dst[:, j * P:(j + 1) * P], src[:, j * P:(j + 1) * P], idn[:])
                last.then_inc(s[name], 1)

            def project(dst, n, name):
                nc.tensor.matmul(dst[:], wproj[:, n, :], xnT[:], start=True, stop=True).then_inc(s[name], 1)

            pe.wait_ge(s["consts_in"], N_CONST)
            pe.wait_ge(s["ones_set"], 1)

            def step(i, par):
                b = i
                c = i - 1
                if on(i, 0):
                    after(pe, "xn_ready", b + 1)
                    after(pe, "g_saved", b)
                    transposes(P0, xn[:].rearrange("p j d -> p (j d)"), "xnT_psum")
                if on(i, 1):
                    o = 1 - par
                    after(pe, "k_rot", c + 1)
                    after(pe, "lep_chain", c * 6)
                    transposes(T1, krot[o][:], "k_tr")
                    after(pe, "v_saved", c + 1)
                    after(pe, "att_ready", c * 2)
                    transposes(N0, vpad[o][:, PAD:PAD + S], "v_tr")
                    nc.tensor.transpose(N1[0:1, 0:P], vsum[o][:], idn[:]).then_inc(s["vs_tr"], 1)
                if on(i, 0):
                    after(pe, "xnT_ready", b + 1)
                    after(pe, "k_sin", b)
                    project(P1, 0, "q_psum")
                    project(P2, 1, "qp_psum")
                if on(i, 3):
                    after(pe, "yn_ready", i - 2)
                    after(pe, "rt", (i - 3) * RT_STEPS)
                    transposes(B1, yn[:].rearrange("p j d -> p (j d)"), "y_tr")
                if on(i, 1):
                    after(pe, "k_tok", c + 1)
                    after(pe, "v_tok", c + 1)
                    after(pe, "ks_masked", c)
                    for j in range(SUB):
                        last = nc.tensor.matmul(KV[:, 0:D + 1], ktok[:, j, :], vtok[:, j, :],
                                                start=(j == 0), stop=(j == SUB - 1))
                    last.then_inc(s["kv_psum"], 1)
                if on(i, 0):
                    project(P0, 2, "k_psum")
                    after(pe, "q_cos", b + 1)
                    project(P1, 3, "kp_psum")
                if on(i, 2):
                    after(pe, "o_ready", i - 1)
                    after(pe, "yT_ready", i - 2)
                    for j in range(SUB):
                        last = nc.tensor.matmul(B1[:, j * D:(j + 1) * D], oT[:, j * P:(j + 1) * P], wo[:],
                                                start=True, stop=True)
                    last.then_inc(s["wo_psum"], 1)
                if on(i, 1):
                    after(pe, "ks_masked", c + 1)
                    after(pe, "v_row", c + 1)
                    for j in range(SUB):
                        dst = NN[j // 2][:, (j % 2) * ND:(j % 2 + 1) * ND]
                        nc.tensor.matmul(dst, qrot[1 - par][:, j * P:(j + 1) * P], kvbd[:], start=True, stop=False)
                        last = nc.tensor.matmul(dst, ones_row[:], vrow[:], start=False, stop=True)
                        if j % 2:
                            last.then_inc(s[f"num{j // 2}"], 1)
                if on(i, 0):
                    after(pe, "q_sin", b + 1)
                    project(P2, 4, "v_psum")
                if on(i, 3):
                    after(pe, "yT_ready", i - 2)
                    if on(i, 2):
                        after(pe, "x2_ready", i - 1)
                    for j in range(SUB):
                        last = nc.tensor.matmul(B1[:, j * E:(j + 1) * E], yT[:, j * P:(j + 1) * P], gateT[:],
                                                start=True, stop=True)
                    last.then_inc(s["gate_psum"], 1)
                if on(i, 0):
                    after(pe, "k_cos", b + 1)
                    project(P0, 5, "g_psum")
                if on(i, 1):
                    after(pe, "att_ready", (c + 1) * 2)
                    transposes(T1, att[:].rearrange("p j d -> p (j d)"), "a_tr")

            pipeline(pe, step)

            HB = [P0, P1]
            YB = [P2, T1]
            pe.wait_ge(s["yT_kept"], NB)
            pe.wait_ge(s["g_saved"], NB)
            pe.wait_ge(s["k_sin"], NB)
            pe.wait_ge(s["v_saved"], NB)
            pe.wait_ge(s["lep_chain"], NB * 6)
            def expert_batch(b):
                after(pe, "cs_ready", b + 1)
                for j in range(SUB):
                    last = nc.tensor.transpose(N0[0:E, j * P:(j + 1) * P], combS[:, j, :], idn[:])
                last.then_inc(s["ct_psum"], 1)
                after(pe, "ct_ready", b + 1)
                after(pe, "acc_ready", b)
                for j in range(SUB):
                    last = nc.tensor.matmul(N1[:, j * D:(j + 1) * D], combT[:, j * P:(j + 1) * P], b2s[:],
                                            start=True, stop=True)
                last.then_inc(s["b2_psum"], 1)
                steps = [(e, c) for e in range(E) for c in range(FC)]

                def yT_of(b):
                    if isinstance(b, int):
                        return yT_all[:, b, :]
                    return yT_all[:, bass.ds(b, 1), :].rearrange("p a s -> p (a s)")

                def up(n):
                    e, c = steps[n]
                    after(pe, "h_ready", b * (E * FC) + max(n - 1, 0))
                    nc.tensor.matmul(HB[n % 2][:], w1s[:, e, c * P:(c + 1) * P], yT_of(b),
                                     start=True, stop=True).then_inc(s["h_psum"], 1)

                def down(n):
                    e, c = steps[n]
                    after(pe, "h_ready", b * (E * FC) + (n + 1))
                    if c == 0:
                        if e >= 2:
                            after(pe, "acc_step", b * (E * SUB) + (e - 1) * SUB)
                        else:
                            after(pe, "acc_step", b * (E * SUB))
                    for j in range(SUB):
                        last = nc.tensor.matmul(YB[e % 2][:, j * D:(j + 1) * D], hS[n % 4][:, j * P:(j + 1) * P],
                                                w2s[:, e, c, :], start=(c == 0 and j == 0), stop=(c == FC - 1),
                                                skip_group_check=True)
                    last.then_inc(s["y_psum"], 1)

                for n in range(len(steps) + 1):
                    if n < len(steps):
                        up(n)
                    if n >= 1:
                        down(n - 1)

            expert_batch(0)
            with pe.Fori(1, NB) as b:
                expert_batch(b)

        @block.scalar
        def _(act):
            act.dma_start(xres[:, 0:SUB * 4, :], x.rearrange("(t p) d -> p t d", p=P)[:, 0:SUB * 4, :]).then_inc(s["x_in"], 16)
            act.dma_start(xres[:, SUB * 4:, :], x.rearrange("(t p) d -> p t d", p=P)[:, SUB * 4:, :]).then_inc(s["x_in"], 16)
            act.wait_ge(s["consts_in"], N_CONST)
            act.wait_ge(s["consts_set"], 1)

            def step(i, par):
                b, c, o = i, i - 1, 1 - par
                if on(i, 0):
                    after(act, "xnT_psum", b + 1)
                    after(act, "g_psum", b)
                    nc.scalar.copy(xnT[:], P0[:]).then_inc(s["xnT_ready"], 1)
                if on(i, 1):
                    after(act, "k_tr", c + 1)
                    after(act, "kv_psum", c)
                    nc.scalar.copy(ktok[:], T1[:].rearrange("p (j d) -> p j d", j=SUB)).then_inc(s["k_tok"], 1)
                    after(act, "v_tr", c + 1)
                    nc.scalar.copy(vtok[:, :, 0:D], N0[:].rearrange("p (j d) -> p j d", j=SUB)).then_inc(s["v_tok"], 1)
                    after(act, "vs_tr", c + 1)
                    after(act, "num1", c)
                    nc.scalar.copy(vrow[0:1, 0:D], N1[0:1, 0:D]).then_inc(s["v_row"], 1)
                if on(i, 3):
                    after(act, "y_tr", i - 2)
                    after(act, "gate_psum", i - 3)
                    after(act, "yT_kept", i - 3)
                    nc.scalar.copy(yT[:], B1[:]).then_inc(s["yT_ready"], 1)
                if on(i, 1):
                    after(act, "o_ready", c)
                    nc.scalar.activation(lep[:], vpad[o][:, 0:S], ACT.Identity, bias=lb[:, 0:1],
                                         scale=lw[:, 0:1]).then_inc(s["lep_chain"], 1)
                if on(i, 0):
                    after(act, "v_psum", b + 1)
                    after(act, "lep_chain", (b - 1) * 6)
                    nc.scalar.activation(vpad[par][:, PAD:PAD + S], P2[:], ACT.Copy,
                                         accum_out=vsum[par][:]).then_inc(s["v_saved"], 1)
                    after(act, "g_psum", b + 1)
                    after(act, "o_ready", b - 1)
                    nc.scalar.copy(gT[par][:], P0[:]).then_inc(s["g_saved"], 1)
                if on(i, 3):
                    after(act, "lg_sub", i - 2)
                    nc.scalar.activation(ex[:], lg[:], ACT.Exp).then_inc(s["ex_ready"], 1)

            pipeline(act, step)

            HB = [P0, P1]
            def expert_batch(b):
                after(act, "ct_psum", b + 1)
                after(act, "b2_psum", b)
                nc.scalar.copy(combT[:], N0[0:E, :]).then_inc(s["ct_ready"], 1)
                for n in range(E * FC):
                    e, c = n // FC, n % FC
                    after(act, "h_psum", b * (E * FC) + (n + 1))
                    if n >= 4:
                        after(act, "y_psum", b * (E * FC) + (n - 3))
                    nc.scalar.activation(hS[n % 4][:], HB[n % 2][:], ACT.Silu, bias=b1s[:, e, c:c + 1]).then_inc(s["h_ready"], 1)

            expert_batch(0)
            with act.Fori(1, NB) as b:
                expert_batch(b)

        @block.gpsimd
        def _(pool):
            nc.gpsimd.memset(half[:], -0.5).then_inc(s["consts_set"], 1)
            nc.gpsimd.memset(ones_row[:], 1.0)
            nc.gpsimd.memset(vtok[:, :, D:D + 1], 1.0)
            nc.gpsimd.memset(vrow[0:1, D:ND], float(S)).then_inc(s["ones_set"], 1)
            pool.wait_ge(s["consts_set"], 1)

            def step(i, par):
                if on(i, 0):
                    b = i
                    after(pool, "q_sin", b + 1)
                    after(pool, "num1", b - 1)
                    nc.gpsimd.tensor_tensor(qrot[par][:], q_c[:], q_s[:], ALU.add).then_inc(s["q_rot"], 1)
                    after(pool, "k_sin", b + 1)
                    after(pool, "k_tr", b - 1)
                    nc.gpsimd.tensor_tensor(krot[par][:], k_c[:], k_s[:], ALU.add).then_inc(s["k_rot"], 1)
                if on(i, 2):
                    after(pool, "ln2_ve", i - 1)
                    nc.gpsimd.tensor_tensor(rs2[:], ve2[:], half[:], ALU.pow).then_inc(s["ln2_rs"], 1)
                if on(i, 3):
                    after(pool, "yT_ready", i - 2)
                    nc.gpsimd.tensor_copy(yT_all[:, i - 3, :] if isinstance(i, int) else yT_all[:, bass.ds(i - 3, 1), :].rearrange("p a s -> p (a s)"), yT[:]).then_inc(s["yT_kept"], 1)
                if on(i, -1):
                    after(pool, "ln1_ve", i + 2)
                    nc.gpsimd.tensor_tensor(rs1[:], ve1[:], half[:], ALU.pow).then_inc(s["ln1_rs"], 1)

            after(pool, "ln1_ve", 1)
            nc.gpsimd.tensor_tensor(rs1[:], ve1[:], half[:], ALU.pow).then_inc(s["ln1_rs"], 1)
            pipeline(pool, step)

            def expert_batch(b):
                after(pool, "rt", NB * RT_STEPS)
                after(pool, "ct_psum", b)
                nc.gpsimd.tensor_copy(combS[:], comb_all[:, bass.ds(b * SUB, SUB), :] if not isinstance(b, int) else comb_all[:, b * SUB:(b + 1) * SUB, :]).then_inc(s["cs_ready"], 1)

            expert_batch(0)
            with pool.Fori(1, NB) as b:
                expert_batch(b)

        @block.vector
        def _(dve):
            for i in range(2):
                nc.vector.memset(vpad[i][:], 0.0)
            nc.vector.memset(rs1[:], 0.0).then_inc(s["consts_set"], 1)
            dve.wait_ge(s["consts_in"], N_CONST)
            dve.wait_ge(s["x_in"], 32)
            dve.wait_ge(s["consts_set"], 2)

            def tile_of(b):
                if isinstance(b, int):
                    return xres[:, b * SUB:(b + 1) * SUB, :]
                return xres[:, bass.ds(b * SUB, SUB), :]

            def xrow(b, j):
                if isinstance(b, int):
                    return xres[:, b * SUB + j, :]
                return xres[:, bass.ds(b * SUB + j, 1), :].rearrange("p a d -> p (a d)")

            def normalise(b, src, st, mv, ve, rs, dst, tag, free_name, free_n, done):
                for j in range(SUB):
                    last = nc.vector.bn_stats(st[:, j, :], src[:, j, :])
                last.then_inc(s[tag + "_stats"], 1)
                after(dve, tag + "_stats", b + 1, alone=True)
                for j in range(SUB):
                    last = nc.vector.bn_aggr(mv[:, j, :], st[:, j, :])
                last.then_inc(s[tag + "_mv"], 1)
                after(dve, tag + "_mv", b + 1)
                after(dve, tag + "_rs", b)
                nc.vector.tensor_scalar(ve[:], mv[:, :, 1], EPS, None, ALU.add).then_inc(s[tag + "_ve"], 1)
                after(dve, tag + "_rs", b + 1)
                after(dve, free_name, free_n)
                for j in range(SUB):
                    last = nc.vector.tensor_scalar(dst[:, j, :], src[:, j, :], mv[:, j, 0:1], rs[:, j:j + 1],
                                                   ALU.subtract, ALU.mult)
                last.then_inc(s[done], 1)

            def ln1(b, par):
                after(dve, f"xin_full{par}", (b - par) * 8 + 16, alone=True)
                normalise(b, xin[par], st1, mv1, ve1, rs1, xn, "ln1", "xnT_psum", b, "xn_ready")

            def rope(b, src_c, src_s, dst_c, dst_s, c_name, s_name, c_done, s_done, free):
                after(dve, c_name, b + 1)
                after(dve, free, b)
                nc.vector.tensor_tensor(dst_c[:], src_c[:], cosT[:], ALU.mult).then_inc(s[c_done], 1)
                after(dve, s_name, b + 1)
                nc.vector.tensor_tensor(dst_s[:], src_s[:], sinT[:], ALU.mult).then_inc(s[s_done], 1)

            def route(b):
                base = b * RT_STEPS
                n = [0]

                def link(ins):
                    n[0] += 1
                    ins.then_inc(s["rt"], 1)
                    after(dve, "rt", base + n[0])

                def bc(ap):
                    return ap[:].unsqueeze(2).to_broadcast([P, SUB, E])

                after(dve, "gate_psum", b + 1)
                logits = B1[:, 0:SUB * E].rearrange("p (j e) -> p j e", j=SUB)
                link(nc.vector.tensor_reduce(red[:], logits, AX_X, ALU.max))
                after(dve, "ex_ready", b)
                nc.vector.tensor_tensor(lg[:], logits, bc(red), ALU.subtract).then_inc(s["lg_sub"], 1)
                after(dve, "ex_ready", b + 1)
                link(nc.vector.tensor_reduce(red[:], ex[:], AX_X, ALU.add))
                link(nc.vector.reciprocal(red[:], red[:]))
                link(nc.vector.tensor_tensor(pr[:], ex[:], bc(red), ALU.mult))

                def pick(src, hot):
                    link(nc.vector.tensor_reduce(red[:], src[:], AX_X, ALU.max))
                    link(nc.vector.tensor_tensor(hot[:], src[:], bc(red), ALU.is_equal))
                    link(nc.vector.tensor_tensor(tmp8[:], hot[:], rankw[:], ALU.mult))
                    link(nc.vector.tensor_reduce(red[:], tmp8[:], AX_X, ALU.max))
                    link(nc.vector.tensor_tensor(hot[:], tmp8[:], bc(red), ALU.is_equal))

                pick(pr, oh1)
                link(nc.vector.scalar_tensor_tensor(tmp8[:], oh1[:], -2.0, pr[:], ALU.mult, ALU.add))
                link(nc.vector.tensor_copy(ex[:], tmp8[:]))
                pick(ex, oh2)
                link(nc.vector.tensor_tensor(oh1[:], oh1[:], oh2[:], ALU.add))
                dst = comb_all[:, b * SUB:(b + 1) * SUB, :] if isinstance(b, int) else comb_all[:, bass.ds(b * SUB, SUB), :]
                link(nc.vector.tensor_tensor(dst, oh1[:], pr[:], ALU.mult))
                assert n[0] == RT_STEPS, n[0]

            def step(i, par):
                b, c, o = i, i - 1, 1 - par
                if on(i, 0):
                    rope(b, P1, P2, q_c, q_s, "q_psum", "qp_psum", "q_cos", "q_sin", "q_rot")
                if on(i, 1):
                    after(dve, "kv_psum", c + 1)
                    after(dve, "num1", c)
                    nc.vector.tensor_tensor(kvbd[:, 0:D], KV[:, 0:D], hmask[:, 0:D], ALU.mult)
                    nc.vector.tensor_scalar(kvbd[:, D:ND], hmask[:, D:ND], KV[:, D:D + 1], None,
                                            ALU.mult).then_inc(s["ks_masked"], 1)
                if on(i, 0):
                    rope(b, P0, P1, k_c, k_s, "k_psum", "kp_psum", "k_cos", "k_sin", "k_rot")
                if on(i, 1):
                    for h in range(2):
                        after(dve, f"num{h}", c + 1)
                        v = NN[h][:, 0:2 * ND].rearrange("p (j n) -> p j n", j=2)
                        nc.vector.reciprocal(rden[:, 2 * h:2 * h + 2, :], v[:, :, D:ND]).then_inc(s["rden_ready"], 1)
                        after(dve, "rden_ready", c * 2 + (h + 1))
                        if h == 0:
                            after(dve, "a_tr", c)
                        nc.vector.tensor_tensor(
                            att[:, 2 * h:2 * h + 2, :].rearrange("p j (h e) -> p j h e", h=H),
                            v[:, :, 0:D].rearrange("p j (h e) -> p j h e", h=H),
                            rden[:, 2 * h:2 * h + 2, :].unsqueeze(3).to_broadcast([P, 2, H, DK]),
                            ALU.mult).then_inc(s["att_ready"], 1)
                if on(i, 2):
                    after(dve, "wo_psum", i - 1)
                    nc.vector.tensor_tensor(x2[:], B1[:].rearrange("p (j d) -> p j d", j=SUB), tile_of(i - 2),
                                            ALU.add).then_inc(s["x2_ready"], 1)
                    after(dve, "x2_ready", i - 1, alone=True)
                    nc.vector.tensor_copy(tile_of(i - 2), x2[:]).then_inc(s["x2_kept"], 1)
                    normalise(i - 2, x2, st2, mv2, ve2, rs2, yn, "ln2", "y_tr", i - 2, "yn_ready")
                if on(i, 3):
                    route(i - 3)
                if on(i, -1):
                    ln1(i + 1, 1 - par)
                if on(i, 1):
                    for t in range(1, TAPS):
                        after(dve, "lep_chain", c * 6 + t)
                        nc.vector.scalar_tensor_tensor(lep[:], vpad[o][:, t:t + S], lw[:, t:t + 1], lep[:],
                                                       ALU.mult, ALU.add).then_inc(s["lep_chain"], 1)
                    after(dve, "lep_chain", c * 6 + TAPS)
                    after(dve, "a_tr", c + 1)
                    nc.vector.tensor_tensor(lep[:], T1[:], lep[:], ALU.add).then_inc(s["lep_chain"], 1)
                    after(dve, "lep_chain", c * 6 + TAPS + 1)
                    after(dve, "wo_psum", c)
                    nc.vector.tensor_tensor(oT[:], lep[:], gT[o][:], ALU.mult).then_inc(s["o_ready"], 1)

            ln1(0, 0)
            pipeline(dve, step)

            YB = [P2, T1]
            dve.wait_ge(s["x2_kept"], NB)
            def expert_batch(b):
                after(dve, "b2_psum", b + 1)
                nc.vector.tensor_tensor(tile_of(b), N1[:].rearrange("p (j d) -> p j d", j=SUB), tile_of(b),
                                        ALU.add).then_inc(s["acc_ready"], 1)
                after(dve, "acc_ready", b + 1)
                for e in range(E):
                    after(dve, "y_psum", b * (E * FC) + (e + 1) * FC)
                    if e:
                        after(dve, "acc_step", b * (E * SUB) + e * SUB)
                    for j in range(SUB):
                        cs = comb_all[:, b * SUB + j, e:e + 1] if isinstance(b, int) else \
                            comb_all[:, bass.ds(b * SUB + j, 1), e:e + 1].rearrange("p a e -> p (a e)")
                        nc.vector.scalar_tensor_tensor(xrow(b, j), YB[e % 2][:, j * D:(j + 1) * D], cs, xrow(b, j),
                                                       ALU.mult, ALU.add).then_inc(s["acc_step"], 1)

            expert_batch(0)
            with dve.Fori(1, NB) as b:
                expert_batch(b)


RT_STEPS = 18

_INS = ["x", "w_proj", "w_o", "cos_t", "sin_t", "head_mask", "ident", "lepe_w", "lepe_b", "gate_t", "rank_w", "w1", "b1", "w2", "b2"]


def rope_tables():
    inv = (np.float32(1.0) / np.float32(10000.0) ** (np.arange(0, DK, 2, dtype=np.float32) / np.float32(DK))).astype(np.float32)
    freqs = np.arange(S, dtype=np.float32)[:, None] * inv[None, :]
    emb = np.concatenate([freqs, freqs], axis=1)
    sign = np.where(np.arange(DK) < DK // 2, -1.0, 1.0).astype(np.float32)
    cos = np.tile(np.cos(emb).astype(np.float32).T, (H, 1))
    sin = np.tile((np.sin(emb).astype(np.float32) * sign[None, :]).T, (H, 1))
    return np.ascontiguousarray(cos), np.ascontiguousarray(sin)


def head_masks():
    head = np.arange(D) // DK
    full = (head[:, None] == head[None, :]).astype(np.float32)
    each = (head[:, None] == np.arange(H)[None, :]).astype(np.float32)
    return np.concatenate([full, each], axis=1) * np.float32(DK ** -0.5)


def kernel(**inputs):
    import concourse.bacc as _bacc
    from concourse.bass_utils import run_bass_kernel_spmd as _run

    g = {n: np.asarray(v) for n, v in inputs.items()}
    rot = np.arange(D).reshape(H, 2, DK // 2)[:, ::-1].reshape(-1)
    wq, wk, wv, wg = (g[f"L0_attn_{n}"] for n in ("Wq", "Wk", "Wv", "Wg"))
    cos, sin = rope_tables()
    lay = {
        "x": g["L0_attn_hidden_states"].reshape(NB * S, D),
        "w_proj": np.stack([wq.T, wq[rot].T, wk.T, wk[rot].T, wv.T, wg.T], axis=1),
        "w_o": g["L0_attn_Wo"].T,
        "cos_t": cos, "sin_t": sin, "head_mask": head_masks(), "ident": np.eye(P, dtype=np.float32),
        "lepe_w": g["L0_attn_lepe_w"].reshape(D, TAPS),
        "lepe_b": g["L0_attn_lepe_b"].reshape(D, 1),
        "gate_t": g["L0_ffn_gate_w"].T,
        "rank_w": np.ascontiguousarray(np.broadcast_to(np.arange(E, 0, -1, dtype=np.float32), (P, SUB, E))),
        "w1": g["L0_ffn_w1"], "b1": g["L0_ffn_b1"].reshape(E, FC, P).transpose(2, 0, 1),
        "w2": g["L0_ffn_w2"], "b2": g["L0_ffn_b2"],
    }
    nc = _bacc.Bacc("TRN2", target_bir_lowering=False, num_devices=1)
    arrays, args = {}, []
    for name in _INS:
        a = np.ascontiguousarray(lay[name])
        arrays[f"in_{name}"] = a
        args.append(nc.dram_tensor(f"in_{name}", a.shape, mybir.dt.from_np(a.dtype), kind="ExternalInput").ap())
    args.append(nc.dram_tensor("out_x", (NB * S, D), F32, kind="ExternalOutput").ap())
    build(nc, *args)
    r = _run(nc, [arrays], core_ids=[0])
    return r.results[0]["out_x"].reshape(NB, S, D)
```

```python
from contextlib import ExitStack

import numpy as np
import concourse.bass as bass
from concourse import mybir

ALU = mybir.AluOpType
ACT = mybir.ActivationFunctionType
F32 = mybir.dt.float32
F32R = mybir.dt.float32r
BF16 = mybir.dt.bfloat16
U32 = mybir.dt.uint32
AX_X = mybir.AxisListType.X

P = 128
NB = 16
S = 512
SUB = S // P
N_TOK = NB * S
D = 128
H = 8
DK = D // H
TAPS = 5
PAD = TAPS // 2
E = 8
TOP_K = 2
F = 512
FC = F // P
EPS = 1e-5
ND = D + H

TS = 512
TSUB = TS // P
CAP = N_TOK + TS
N_TILES = (TOP_K * N_TOK + E * (TS - 1)) // TS
W_AT, ID_AT = D, D + E
ROW = D + E + 1
WPACK = 2 * F
BPACK = FC + 1 + E
NBUF = 3
DOWN_LAG = 2
N_COUNT = N_TOK // TS

LEAD, LAG = 2, 6
LOOP_FROM, LOOP_TO = 6, 11

N_PROJ = 5
FIRST = {"w_proj": N_PROJ * D, "ident": P}
SECOND = {"lepe_rows": TAPS * D, "cos_t": S, "sin_t": S, "head_mask": ND, "w_o": D, "lepe_b": 1, "gate_t": E,
          "rank_w": SUB * E, "region": SUB * E, "before": P, "ids": NB * SUB}


def build(nc, x, first, second, tables_k, tail_rows, row_consts, w_experts, b_experts, out):
    rows_in = nc.dram_tensor("rows_in", (E * CAP + TS, ROW), F32, kind="Internal").ap()

    with ExitStack() as ctx:
        def sb(name, shape, dt=F32):
            return ctx.enter_context(nc.sbuf_tensor(name, shape, dt))

        def bank(name, n=1):
            return ctx.enter_context(nc.psum_tensor(name, [P, n * 512], F32))

        def sem(name):
            return ctx.enter_context(nc.semaphore(name))

        first_sb = sb("first_sb", [P, sum(FIRST.values())])
        second_sb = sb("second_sb", [P, sum(SECOND.values())])

        def part(whole, widths, name):
            names = list(widths)
            at = sum(widths[n] for n in names[:names.index(name)])
            return whole[:, at:at + widths[name]]

        wproj = part(first_sb, FIRST, "w_proj").rearrange("p (n d) -> p n d", n=N_PROJ)
        idn = part(first_sb, FIRST, "ident")
        lrows = part(second_sb, SECOND, "lepe_rows").rearrange("p (t d) -> p t d", t=TAPS)
        cosT = part(second_sb, SECOND, "cos_t")
        sinT = part(second_sb, SECOND, "sin_t")
        hmask = part(second_sb, SECOND, "head_mask")
        wo = part(second_sb, SECOND, "w_o")
        lb = part(second_sb, SECOND, "lepe_b")
        gateT = part(second_sb, SECOND, "gate_t")
        rankw = part(second_sb, SECOND, "rank_w").rearrange("p (j e) -> p j e", j=SUB)
        reg0 = part(second_sb, SECOND, "region").rearrange("p (j e) -> p j e", j=SUB)
        bef = part(second_sb, SECOND, "before")
        ids = part(second_sb, SECOND, "ids")
        wproj_h = sb("wproj_h", [P, N_PROJ, D], F32R)
        wproj_l = sb("wproj_l", [P, N_PROJ, D], F32R)
        wconv = sb("wconv", [P, TAPS, D])
        wconv_h = sb("wconv_h", [P, TAPS, D], F32R)
        wconv_l = sb("wconv_l", [P, TAPS, D], F32R)
        bef16 = sb("bef16", [P, P], BF16)
        one16 = sb("one16", [P, P], BF16)
        half = sb("half", [P, 2 * SUB])
        ones_row = sb("ones_row", [1, P])
        consts_row = sb("consts_row", [1, E * N_COUNT + E * E + N_TILES * E])
        thr = consts_row[:, 0:E * N_COUNT].rearrange("p (e n) -> p e n", e=E)
        cumu = consts_row[:, E * N_COUNT:E * N_COUNT + E * E].rearrange("p (e f) -> p e f", e=E)
        tno = consts_row[:, E * N_COUNT + E * E:].rearrange("p (t e) -> p t e", e=E)
        tail = sb("tail", [P, TSUB, ROW])

        wres = sb("wres", [P, E, 2, WPACK], F32R)
        bres = sb("bres", [P, E, BPACK])

        st = sb("st", [P, 2 * SUB, 6])
        mv = [sb(f"mv{i}", [P, 2 * SUB, 2]) for i in range(2)]
        ve = sb("ve", [P, 2 * SUB])
        rs = [sb(f"rs{i}", [P, 2 * SUB]) for i in range(2)]
        nb = [sb(f"nb{i}", [P, 2 * SUB]) for i in range(2)]

        lgs = sb("lgs", [P, SUB, E])
        lg = sb("lg", [P, SUB, E])
        ex = sb("ex", [P, SUB, E])
        pr = sb("pr", [P, SUB, E])
        pr2 = sb("pr2", [P, SUB, E])
        oh = sb("oh", [P, TOP_K, SUB, E])
        ohs = sb("ohs", [P, SUB, E])
        oh16 = sb("oh16", [P, SUB, E], BF16)
        tmp8 = sb("tmp8", [P, SUB, E])
        tmp16 = sb("tmp16", [P, TOP_K, SUB, E])
        red = sb("red", [P, SUB])
        msum = sb("msum", [P, E])
        macc = sb("macc", [P, E])
        macc16 = sb("macc16", [P, E], BF16)
        rk = sb("rk", [P, SUB, E])
        slot_f = sb("slot_f", [P, TOP_K, SUB])
        slots = [sb(f"slots{i}", [P, TOP_K, SUB], U32) for i in range(2)]

        cnt = sb("cnt", [1, E])
        fill_at = sb("fill_at", [1, E], U32)
        gt = sb("gt", [1, E, N_COUNT])
        ntile = sb("ntile", [1, E])
        cm = sb("cm", [1, E, E])
        incl = sb("incl", [1, E])
        skip = sb("skip", [1, E])
        passed = sb("passed", [1, N_TILES, E])
        pskip = sb("pskip", [1, N_TILES, E])
        trow_f = sb("trow_f", [1, N_TILES])
        texp_f = sb("texp_f", [1, N_TILES])
        trow = sb("trow", [1, N_TILES], U32)
        texp = sb("texp", [1, N_TILES], U32)

        attention = ExitStack()

        def sa(name, shape, dt=F32):
            return attention.enter_context(nc.sbuf_tensor(name, shape, dt))

        wraw = [sa(f"wraw{i}", [P, WPACK]) for i in range(2)]
        xin = [sa(f"xin{i}", [P, SUB, D]) for i in range(2)]
        xre = [sa(f"xre{i}", [P, SUB, D]) for i in range(2)]
        xn = sa("xn", [P, SUB, D])
        xnT_h = [sa(f"xnT_h{i}", [P, S + 2 * PAD], F32R) for i in range(2)]
        xnT_l = [sa(f"xnT_l{i}", [P, S + 2 * PAD], F32R) for i in range(2)]
        tabk = sa("tabk", [P, 2, SUB, D])
        q_c = sa("q_c", [P, S])
        q_s = sa("q_s", [P, S])
        k_c = sa("k_c", [P, SUB, D])
        k_s = sa("k_s", [P, SUB, D])
        qrot = [sa(f"qrot{i}", [P, S]) for i in range(2)]
        ktok = sa("ktok", [P, SUB, D])
        vtok = sa("vtok", [P, SUB, D + 1])
        gT = [sa(f"gT{i}", [P, S]) for i in range(2)]
        vcol = sa("vcol", [P, 1])
        vrow = sa("vrow", [1, ND])
        kvbd = sa("kvbd", [P, ND])
        rden = sa("rden", [P, SUB, H])
        att = sa("att", [P, SUB, D])
        oT = sa("oT", [P, S])
        x2 = [sa(f"x2{i}", [P, SUB, D]) for i in range(2)]
        yn = sa("yn", [P, SUB, D])
        yT = sa("yT", [P, S])
        yall = sa("yall", [P, NB * SUB, ROW])
        yout = [sa(f"yout{i}", [P, SUB, ROW]) for i in range(2)]
        attention.close()

        xg = [sb(f"xg{i}", [P, TSUB, ROW]) for i in range(NBUF)]
        wst = [sb(f"wst{i}", [P, 2, WPACK], F32R) for i in range(NBUF)]
        bst = [sb(f"bst{i}", [P, BPACK]) for i in range(NBUF)]
        xT_h = [sb(f"xT_h{i}", [P, TS], F32R) for i in range(NBUF)]
        xT_l = [sb(f"xT_l{i}", [P, TS], F32R) for i in range(NBUF)]
        wsel = sb("wsel", [P, TSUB, E])
        wv = [sb(f"wv{i}", [P, TSUB]) for i in range(NBUF)]
        tok_f = [sb(f"tok_f{i}", [P, TSUB]) for i in range(NBUF)]
        tok = [sb(f"tok{i}", [P, TSUB], U32) for i in range(NBUF)]
        hf = [sb(f"hf{i}", [P, TS]) for i in range(FC)]
        hh = [sb(f"hh{i}", [P, TS], F32R) for i in range(FC)]
        hl = [sb(f"hl{i}", [P, TS], F32R) for i in range(FC)]
        yTs = sb("yTs", [P, TS])
        yo = [sb(f"yo{i}", [P, TSUB, D]) for i in range(NBUF)]

        qp = bank("qp", 2)
        kvp = bank("kvp", 2)
        KV, CV, GW, XB = [bank(n) for n in ("kv", "conv", "gate_wo", "rows")]
        VS_AT, VR_AT = D + 2, 2 * D
        HB, YB, TY = [qp[:, 0:512], qp[:, 512:1024], kvp[:, 0:512]], [kvp[:, 512:1024], KV, CV], GW

        names = """first_in second_in tabk_in tail_in rowc_in wraw_in0 wraw_in1 bres_in xin_full0 xin_full1 xre_full0 xre_full1
            consts_set ones_set wsplit w_high w_low bef_set
            stats mv_ready ve_ready ln_rs nb_ready xn_ready xnT_psum xnTh_ready xnTl_ready
            q_psum qp_psum q_cos q_sin q_rot kvp_psum k_cos k_sin ktok_ready vtok_ready g_psum g_saved
            kv_psum vs_psum vcol_ready vs_tr v_row ks_masked num_psum rden_ready att_ready a_tr o_ready
            wo_psum x2_ready x2_out0 x2_out1 yn_ready y_kept w_kept y_out y_tr yT_ready gate_psum lgs_ready
            lg_sub ex_ready rt oh_ready rank_psum rk_read slots_ready scat0 scat1 cnt_psum fill_ready tb table_ready
            tails_in dummy_in out_dummy
            xg_in0 xg_in1 xg_in2 wst_in0 wst_in1 wst_in2 bst_in0 bst_in1 bst_in2 x_tr xTh_ready xTl_ready wsel_ready wv_ready
            h_psum h_silu h_high h_low y_psum yT_saved yo_tr yo_ready acc_done""".split()
        s = {n: sem(n) for n in names}

        def after(eng, name, n, alone=False):
            if isinstance(n, int) and n <= 0:
                return
            eng.wait_ge(s[name], n)
            if alone:
                eng.nop(nofuse=True)

        block = ctx.enter_context(nc.Block())

        def hbank(t, c):
            return HB[(t.buf * FC + c) % len(HB)]

        def has_ln(i):
            return on(i, -2) or on(i, 2)

        def pipeline(eng, step):
            for i in range(-LEAD, LOOP_FROM):
                step(i, i % 2)
            with eng.Fori(LOOP_FROM, LOOP_TO, 2) as i:
                step(i, 0)
                step(i + 1, 1)
            for i in range(LOOP_TO + 1, NB + LAG):
                step(i, i % 2)

        def on(i, lag):
            return not isinstance(i, int) or 0 <= i - lag < NB

        def all_of(n):
            return min(n, NB) if isinstance(n, int) else n

        class Tile:
            def __init__(self, g, k):
                self.no, self.buf, self.fills = g * NBUF + k, k, g + 1
                self.at = lambda d: Tile(g + (k + d) // NBUF, (k + d) % NBUF)
                self.real = not isinstance(g, int) or 0 <= self.no < N_TILES

        def tile_pipeline(eng, step, extra):
            rounds = N_TILES // NBUF
            assert rounds * NBUF == N_TILES
            for i in range(2 * NBUF):
                step(Tile(i // NBUF, i % NBUF))
            with eng.Fori(2, rounds - 1) as g:
                for k in range(NBUF):
                    step(Tile(g, k))
            for i in range((rounds - 1) * NBUF, N_TILES + extra):
                step(Tile(i // NBUF, i % NBUF))

        xv = x.rearrange("(b j p) d -> p (b j) d", p=P, j=SUB)
        ov = out[0:N_TOK, :].rearrange("(b j p) d -> p (b j) d", p=P, j=SUB)

        def subtiles(b):
            return slice(b * SUB, (b + 1) * SUB) if isinstance(b, int) else bass.ds(b * SUB, SUB)

        def batch(v, b):
            return v[:, subtiles(b), :]

        @block.sync
        def _(sp):
            sp.dma_start(xin[0][:], batch(xv, 0)).then_inc(s["xin_full0"], 16)
            sp.dma_start(first_sb[:], first).then_inc(s["first_in"], 16)
            sp.dma_start(xin[1][:], batch(xv, 1)).then_inc(s["xin_full1"], 16)
            sp.dma_start(second_sb[:], second).then_inc(s["second_in"], 16)
            sp.dma_start(tabk[:], tables_k).then_inc(s["tabk_in"], 16)
            sp.dma_start(tail[:], tail_rows).then_inc(s["tail_in"], 16)
            sp.dma_start(consts_row[:], row_consts).then_inc(s["rowc_in"], 16)
            sp.dma_start(bres[:], b_experts).then_inc(s["bres_in"], 16)

            def load_expert(e):
                after(sp, "w_low", e - 1)
                sp.dma_start(wraw[e % 2][:], w_experts[e]).then_inc(s[f"wraw_in{e % 2}"], 16)

            load_expert(0)
            load_expert(1)
            sp.wait_ge(s["tail_in"], 16)
            sp.dma_start(rows_in[E * CAP:E * CAP + TS, :].rearrange("(p j) w -> p j w", p=P), tail[:]).then_inc(s["dummy_in"], 16)
            sp.dma_start(out[N_TOK:N_TOK + TS, :].rearrange("(p j) d -> p j d", p=P), tail[:, :, 0:D]).then_inc(s["out_dummy"], 16)

            def step(i, par):
                if on(i, 1):
                    after(sp, "x2_ready", i - 2)
                    sp.dma_start(xre[1 - par][:], batch(xv, i - 1)).then_inc(s[f"xre_full{1 - par}"], 16)
                if on(i, -3) and (not isinstance(i, int) or i > -2):
                    after(sp, "xn_ready", i + 2)
                    sp.dma_start(xin[1 - par][:], batch(xv, i + 3)).then_inc(s[f"xin_full{1 - par}"], 16)
                if isinstance(i, int) and 0 <= i + 1 and i + 3 < E:
                    load_expert(i + 3)
                if on(i, 2):
                    after(sp, "x2_ready", i - 1)
                    sp.dma_start(batch(ov, i - 2), x2[par][:]).then_inc(s[f"x2_out{par}"], 16)

            pipeline(sp, step)

            sp.wait_ge(s["fill_ready"], 1)
            for e in range(E):
                r = sp.value_load(fill_at[0:1, e:e + 1], min_val=e * CAP, max_val=e * CAP + N_TOK)
                sp.dma_start(rows_in[bass.ds(r, TS), :].rearrange("(p j) w -> p j w", p=P), tail[:]).then_inc(s["tails_in"], 16)
            sp.wait_ge(s["table_ready"], 2)
            sp.wait_ge(s["tails_in"], E * 16)
            sp.wait_ge(s["dummy_in"], 16)
            sp.wait_ge(s["scat0"], NB // 2 * SUB * TOP_K * 16)
            sp.wait_ge(s["scat1"], NB // 2 * SUB * TOP_K * 16)
            sp.wait_ge(s["w_low"], E)
            sp.wait_ge(s["bres_in"], 16)

            def at(t):
                return slice(t.no, t.no + 1) if isinstance(t.no, int) else bass.ds(t.no, 1)

            def load_rows(t):
                r = sp.value_load(trow[0:1, at(t)], min_val=0, max_val=E * CAP)
                after(sp, "x_tr", t.no - 2)
                after(sp, "wv_ready", t.no - 2)
                sp.dma_start(xg[t.buf][:], rows_in[bass.ds(r, TS), :].rearrange("(p j) w -> p j w", p=P)
                             ).then_inc(s[f"xg_in{t.buf}"], 16)

            def load_tile(t):
                if t.at(1).real:
                    load_rows(t.at(1))
                e = sp.value_load(texp[0:1, at(t)], min_val=0, max_val=E - 1)
                after(sp, "y_psum", t.no - 2)
                sp.dma_start(wst[t.buf][:].bitcast(F32),
                             wres[:, bass.ds(e, 1), :, :].rearrange("p a t w -> p (a t) w").bitcast(F32)
                             ).then_inc(s[f"wst_in{t.buf}"], 16)
                after(sp, "yT_saved", t.no - 2)
                sp.dma_start(bst[t.buf][:], bres[:, bass.ds(e, 1), :].rearrange("p a w -> p (a w)")
                             ).then_inc(s[f"bst_in{t.buf}"], 16)

            load_rows(Tile(0, 0))
            tile_pipeline(sp, load_tile, 0)
            sp.wait_ge(s["acc_done"], N_TILES * TSUB * 16)

        @block.tensor
        def _(pe):
            def transposes(dst, src, name):
                for j in range(SUB):
                    last = nc.tensor.transpose(dst[:, j * P:(j + 1) * P], src(j), idn)
                last.then_inc(s[name], 1)

            def product(dst, w_h, w_l, r_h, r_l, first, last):
                nc.tensor.matmul(dst, w_h, r_h, start=first, stop=False)
                nc.tensor.matmul(dst, w_l, r_h, start=False, stop=False)
                return nc.tensor.matmul(dst, w_h, r_l, start=False, stop=last)

            def project(dst, n, par, name):
                product(dst, wproj_h[:, n, :], wproj_l[:, n, :], xnT_h[par][:, PAD:PAD + S], xnT_l[par][:, PAD:PAD + S],
                        True, True).then_inc(s[name], 1)

            pe.wait_ge(s["first_in"], 16)
            pe.wait_ge(s["second_in"], 16)
            pe.wait_ge(s["ones_set"], 1)
            pe.wait_ge(s["wsplit"], 5)
            pe.wait_ge(s["bef_set"], 1)

            def step(i, par):
                b, c, o = i, i - 1, 1 - par
                if on(i, 1):
                    after(pe, "ktok_ready", c + 1)
                    after(pe, "vtok_ready", c + 1)
                    after(pe, "ks_masked", c)
                    after(pe, "v_row", c)
                    for j in range(SUB):
                        last = nc.tensor.matmul(KV[:, 0:D + 1], ktok[:, j, :], vtok[:, j, :],
                                                start=(j == 0), stop=(j == SUB - 1))
                    last.then_inc(s["kv_psum"], 1)
                    for j in range(SUB):
                        last = nc.tensor.matmul(KV[:, VS_AT:VS_AT + 1], vtok[:, j, 0:D], vtok[:, j, D:D + 1],
                                                start=(j == 0), stop=(j == SUB - 1))
                    last.then_inc(s["vs_psum"], 1)
                if on(i, 0):
                    after(pe, "xnTl_ready", b + 1)
                    after(pe, "att_ready", b - 1)
                    project(qp[:, 0:512], 0, par, "q_psum")
                    project(qp[:, 512:1024], 1, par, "qp_psum")
                if on(i, 2):
                    after(pe, "o_ready", i - 1)
                    after(pe, "rk_read", i - 4)
                    after(pe, "g_saved", all_of(i))
                    for j in range(SUB):
                        last = nc.tensor.matmul(GW[:, j * D:(j + 1) * D], oT[:, j * P:(j + 1) * P], wo,
                                                start=True, stop=True)
                    last.then_inc(s["wo_psum"], 1)
                if on(i, 1):
                    after(pe, "vcol_ready", c + 1)
                    nc.tensor.transpose(KV[0:1, VR_AT:VR_AT + D], vcol[:], idn).then_inc(s["vs_tr"], 1)
                if on(i, 0):
                    after(pe, "k_sin", b)
                    for j in range(SUB):
                        rows = slice(PAD + j * P, PAD + (j + 1) * P)
                        dst = kvp[:, 2 * j * D:2 * (j + 1) * D]
                        nc.tensor.matmul(dst, xnT_h[par][:, rows], wproj_h[:, 3:5, :], start=True, stop=False)
                        nc.tensor.matmul(dst, xnT_h[par][:, rows], wproj_l[:, 3:5, :], start=False, stop=False)
                        last = nc.tensor.matmul(dst, xnT_l[par][:, rows], wproj_h[:, 3:5, :], start=False, stop=True)
                    last.then_inc(s["kvp_psum"], 1)
                if on(i, 1):
                    after(pe, "ks_masked", c + 1)
                    after(pe, "v_row", c + 1)
                    after(pe, "q_rot", c + 1)
                    if on(i, 0):
                        after(pe, "q_sin", b + 1)
                    for j in range(SUB):
                        at = j // 2 * 512 + j % 2 * ND
                        nc.tensor.matmul(qp[:, at:at + ND], qrot[o][:, j * P:(j + 1) * P], kvbd[:], start=True, stop=False)
                        last = nc.tensor.matmul(qp[:, at:at + ND], ones_row[:], vrow[:], start=False, stop=True)
                    last.then_inc(s["num_psum"], 1)
                if on(i, 3):
                    after(pe, "yn_ready", i - 2)
                    after(pe, "xnTl_ready", all_of(i + 1))
                    transposes(XB, lambda j: yn[:, j, :], "y_tr")
                if on(i, 0):
                    if on(i, 2):
                        after(pe, "x2_ready", i - 1)
                    project(GW[:], 2, par, "g_psum")
                if on(i, 3):
                    after(pe, "yT_ready", i - 2)
                    for j in range(SUB):
                        last = nc.tensor.matmul(XB[:, j * E:(j + 1) * E], yT[:, j * P:(j + 1) * P], gateT,
                                                start=True, stop=True)
                    last.then_inc(s["gate_psum"], 1)
                if on(i, 1):
                    after(pe, "o_ready", c)
                    for t in range(TAPS):
                        product(CV[:], wconv_h[:, t, :], wconv_l[:, t, :], xnT_h[o][:, t:t + S], xnT_l[o][:, t:t + S],
                                t == 0, t == TAPS - 1)
                if on(i, 1):
                    after(pe, "att_ready", c + 1)
                    for j in range(SUB):
                        last = nc.tensor.matmul(CV[:, j * P:(j + 1) * P], att[:, j, :], idn, start=False, stop=True,
                                                skip_group_check=True)
                    last.then_inc(s["a_tr"], 1)
                if on(i, -1):
                    after(pe, "xn_ready", i + 2)
                    if on(i, 3):
                        after(pe, "lgs_ready", i - 2)
                    transposes(XB, lambda j: xn[:, j, :], "xnT_psum")
                if on(i, 4):
                    after(pe, "oh_ready", i - 3)
                    after(pe, "g_saved", all_of(i + 1))
                    after(pe, "x2_ready", all_of(i - 1))
                    for j in range(SUB):
                        dst = GW[:, j * E:(j + 1) * E]
                        nc.tensor.matmul(dst, bef16[:], oh16[:, j, :], start=True, stop=False)
                        for k in range(j):
                            nc.tensor.matmul(dst, one16[:], oh16[:, k, :], start=False, stop=False)
                        last = nc.tensor.matmul(dst, one16[:], macc16[:], start=False, stop=True)
                    last.then_inc(s["rank_psum"], 1)

            pipeline(pe, step)
            pe.wait_ge(s["slots_ready"], NB)
            nc.tensor.matmul(GW[:, 0:E], one16[:], macc16[:], start=True, stop=True).then_inc(s["cnt_psum"], 1)

            def rows_to_features(t):
                after(pe, f"xg_in{t.buf}", t.fills * 16)
                after(pe, "xTl_ready", t.no)
                transposes(XB, lambda j: xg[t.buf][:, j, 0:D], "x_tr")

            def up(t, c):
                n = t.no * FC + c
                if c == 0:
                    after(pe, f"wst_in{t.buf}", t.fills * 16)
                    after(pe, "xTl_ready", t.no + 1)
                after(pe, "h_silu", n - len(HB) + 1)
                product(hbank(t, c)[:], wst[t.buf][:, 0, c * P:(c + 1) * P], wst[t.buf][:, 1, c * P:(c + 1) * P],
                        xT_h[t.buf][:], xT_l[t.buf][:], True, True).then_inc(s["h_psum"], 1)

            def down(t, c):
                if c == 0:
                    after(pe, "yT_saved", t.no - NBUF + 1)
                after(pe, "h_low", t.no * FC + c + 1)
                m = product(YB[t.buf][:], wst[t.buf][:, 0, F + c * D:F + (c + 1) * D],
                            wst[t.buf][:, 1, F + c * D:F + (c + 1) * D], hh[c][:], hl[c][:], c == 0, c == FC - 1)
                if c == FC - 1:
                    m.then_inc(s["y_psum"], 1)

            def features_to_rows(t):
                after(pe, "yT_saved", t.no + 1)
                after(pe, "yo_ready", t.no)
                transposes(TY, lambda j: yTs[:, j * P:(j + 1) * P], "yo_tr")

            for name in ("att_ready", "k_sin", "vtok_ready", "ks_masked", "v_row", "o_ready", "xnTl_ready", "lgs_ready"):
                pe.wait_ge(s[name], NB)
            pe.wait_ge(s["fill_ready"], 1)
            rows_to_features(Tile(0, 0))

            def tile_step(t):
                before, behind = t.at(-1), t.at(1)
                for c in range(FC):
                    if t.real:
                        up(t, c)
                    if c < DOWN_LAG:
                        if before.real:
                            down(before, c + FC - DOWN_LAG)
                    elif t.real:
                        down(t, c - DOWN_LAG)
                    if c == 1 and behind.real:
                        rows_to_features(behind)
                if before.real:
                    features_to_rows(before)

            tile_pipeline(pe, tile_step, 1)

        @block.scalar
        def _(act):
            act.wait_ge(s["consts_set"], 2)
            act.wait_ge(s["ones_set"], 1)

            def split_high(e):
                after(act, f"wraw_in{e % 2}", (e // 2 + 1) * 16)
                nc.scalar.copy(wres[:, e, 0, :], wraw[e % 2][:]).then_inc(s["w_high"], 1)

            def apply(dst, src, at, o, done):
                for j in range(SUB):
                    last = nc.scalar.activation(dst[:, j, :], src[:, j, :], ACT.Identity, bias=nb[o][:, at + j:at + j + 1],
                                                scale=rs[o][:, at + j:at + j + 1])
                last.then_inc(s[done], 1)

            def step(i, par):
                b, c, e, o = i, i - 1, i - 3, 1 - par
                if on(i, -1):
                    after(act, "nb_ready", i + 2, alone=True)
                    after(act, "xnT_psum", i + 1)
                    apply(xn, xin[o], 0, o, "xn_ready")
                if on(i, 5):
                    after(act, "w_kept", i - 4)
                    after(act, "y_kept", i - 4)
                    if not isinstance(i, int) or i - 5 > 1:
                        after(act, f"scat{o}", (i - 5 - o) * (SUB * TOP_K * 8))
                    nc.scalar.copy(yout[o][:], yall[:, subtiles(i - 5), :]).then_inc(s["y_out"], 1)
                if on(i, 1):
                    after(act, "ks_masked", c + 1)
                    after(act, "vs_tr", c)
                    nc.scalar.copy(vcol[:], KV[:, VS_AT:VS_AT + 1]).then_inc(s["vcol_ready"], 1)
                if on(i, 3):
                    after(act, "nb_ready", i + 2, alone=True)
                    after(act, "y_kept", e, alone=True)
                    after(act, "y_tr", e)
                    apply(yn, x2[o], SUB, o, "yn_ready")
                if on(i, 1):
                    after(act, "vs_tr", c + 1)
                    after(act, "num_psum", c)
                    nc.scalar.copy(vrow[0:1, 0:D], KV[0:1, VR_AT:VR_AT + D]).then_inc(s["v_row"], 1)
                if on(i, 3):
                    after(act, "yn_ready", e + 1)
                    nc.scalar.copy(yall[:, subtiles(e), 0:D], yn[:]).then_inc(s["y_kept"], 1)
                if on(i, 3):
                    after(act, "y_tr", e + 1)
                    after(act, "gate_psum", e)
                    nc.scalar.copy(yT[:], XB[:]).then_inc(s["yT_ready"], 1)
                if on(i, 0):
                    after(act, "k_sin", b + 1)
                    after(act, "vs_psum", b)
                    nc.scalar.copy(vtok[:, :, 0:D], kvp[:].rearrange("p (j c) -> p j c", j=SUB)[:, :, D:2 * D]
                                   ).then_inc(s["vtok_ready"], 1)
                if on(i, 4):
                    after(act, "lg_sub", i - 3)
                    nc.scalar.activation(ex[:], lg[:], ACT.Exp).then_inc(s["ex_ready"], 1)
                if on(i, 0):
                    after(act, "g_psum", b + 1)
                    after(act, "o_ready", b - 1)
                    nc.scalar.copy(gT[par][:], GW[:]).then_inc(s["g_saved"], 1)
                if on(i, 3):
                    after(act, "gate_psum", e + 1)
                    after(act, "lg_sub", e)
                    nc.scalar.copy(lgs[:], XB[:, 0:SUB * E].rearrange("p (j e) -> p j e", j=SUB)).then_inc(s["lgs_ready"], 1)
                if isinstance(i, int) and i + 2 < E:
                    split_high(i + 2)
                if on(i, -1):
                    after(act, "xnT_psum", i + 2)
                    after(act, "a_tr", i)
                    nc.scalar.copy(xnT_h[o][:, PAD:PAD + S], XB[:]).then_inc(s["xnTh_ready"], 1)

            pipeline(act, step)

            def x_high(t):
                after(act, "x_tr", t.no + 1)
                after(act, "h_psum", (t.no - 2) * FC)
                nc.scalar.copy(xT_h[t.buf][:], XB[:]).then_inc(s["xTh_ready"], 1)

            def tile_step(t):
                before, behind = t.at(-1), t.at(1)
                for c in range(FC):
                    if t.real:
                        n = t.no * FC + c
                        if c == 0:
                            after(act, f"bst_in{t.buf}", t.fills * 16, alone=True)
                        after(act, "h_psum", n + 1, alone=True)
                        after(act, "h_low", n - FC + 1)
                        nc.scalar.activation(hf[c][:], hbank(t, c)[:], ACT.Silu, bias=bst[t.buf][:, c:c + 1]).then_inc(s["h_silu"], 1)
                    if c == 1 and behind.real:
                        x_high(behind)
                    if c == DOWN_LAG and before.real:
                        after(act, "y_psum", before.no + 1, alone=True)
                        after(act, "yo_tr", before.no)
                        nc.scalar.activation(yTs[:], YB[before.buf][:], ACT.Identity,
                                             bias=bst[before.buf][:, FC:FC + 1]).then_inc(s["yT_saved"], 1)

            x_high(Tile(0, 0))
            tile_pipeline(act, tile_step, 1)

        @block.gpsimd
        def _(pool):
            nc.gpsimd.memset(half[:], -0.5).then_inc(s["consts_set"], 1)
            nc.gpsimd.memset(ones_row[:], 1.0)
            nc.gpsimd.memset(one16[:], 1.0)
            nc.gpsimd.memset(vtok[:, :, D:D + 1], 1.0)
            nc.gpsimd.memset(vrow[0:1, D:ND], float(S)).then_inc(s["ones_set"], 1)
            pool.wait_ge(s["consts_set"], 1)

            def split_low(e):
                after(pool, "w_high", e + 1)
                nc.gpsimd.tensor_tensor(wres[:, e, 1, :], wraw[e % 2][:], wres[:, e, 0, :].bitcast(F32),
                                        ALU.subtract).then_inc(s["w_low"], 1)

            def scatter(f, o, k):
                for j in range(SUB):
                    nc.gpsimd.indirect_dma_start(
                        rows_in, bass.IndirectOffsetOnAxis(ap=slots[o][:, k, j:j + 1], axis=0),
                        yout[o][:, j, :], None).then_inc(s[f"scat{o}"], 16)

            def step(i, par):
                b, f, o = i, i - 5, 1 - par
                if on(i, 5):
                    after(pool, "y_out", f + 1, alone=True)
                    after(pool, "slots_ready", f + 1, alone=True)
                    scatter(f, o, 0)
                if on(i, 0):
                    after(pool, "q_sin", b + 1)
                    after(pool, "num_psum", b - 1)
                    nc.gpsimd.tensor_tensor(qrot[par][:], q_c[:], q_s[:], ALU.add).then_inc(s["q_rot"], 1)
                    after(pool, "k_sin", b + 1)
                    after(pool, "kv_psum", b)
                    nc.gpsimd.tensor_tensor(ktok[:], k_c[:], k_s[:], ALU.add).then_inc(s["ktok_ready"], 1)
                if on(i, 5):
                    scatter(f, o, 1)
                if has_ln(i):
                    after(pool, "ve_ready", i + 3)
                    after(pool, "xn_ready", all_of(i + 1))
                    after(pool, "yn_ready", i - 3)
                    nc.gpsimd.tensor_tensor(rs[par][:], ve[:], half[:], ALU.pow).then_inc(s["ln_rs"], 1)
                if isinstance(i, int) and i + 2 < E:
                    split_low(i + 2)

            pipeline(pool, step)

            pool.wait_ge(s["x2_out0"], NB // 2 * 16)
            pool.wait_ge(s["x2_out1"], NB // 2 * 16)
            pool.wait_ge(s["out_dummy"], 16)

            def tile_step(t):
                after(pool, "yo_ready", t.no + 1, alone=True)
                after(pool, "acc_done", t.no * (TSUB * 16), alone=True)
                for j in range(TSUB):
                    nc.gpsimd.indirect_dma_start(
                        out, bass.IndirectOffsetOnAxis(ap=tok[t.buf][:, j:j + 1], axis=0),
                        yo[t.buf][:, j, :], None, compute_op=ALU.add).then_inc(s["acc_done"], 16)

            tile_pipeline(pool, tile_step, 0)

        @block.vector
        def _(dve):
            for i in range(2):
                nc.vector.memset(xnT_h[i][:].bitcast(F32), 0.0)
                nc.vector.memset(xnT_l[i][:].bitcast(F32), 0.0)
            for i in range(2):
                nc.vector.memset(mv[i][:], 0.0)
            nc.vector.memset(macc[:], 0.0)
            nc.vector.memset(macc16[:], 0.0).then_inc(s["consts_set"], 1)
            dve.wait_ge(s["consts_set"], 2)

            def stats(src, at):
                for j in range(SUB):
                    last = nc.vector.bn_stats(st[:, at + j, :], src[:, j, :])
                return last

            def bc(ap):
                return ap[:].unsqueeze(2).to_broadcast([P, SUB, E])

            def chain(n):
                done = [n]

                def link(ins):
                    done[0] = done[0] + 1
                    ins.then_inc(s["rt"], 1)
                    after(dve, "rt", done[0])
                return link

            def shift_logits(b):
                link = chain(b * RT_STEPS)
                after(dve, "lgs_ready", b + 1)
                link(nc.vector.tensor_reduce(red[:], lgs[:], AX_X, ALU.max))
                after(dve, "ex_ready", b)
                nc.vector.tensor_tensor(lg[:], lgs[:], bc(red), ALU.subtract).then_inc(s["lg_sub"], 1)

            def choose(b):
                link = chain(b * RT_STEPS + 1)
                after(dve, "ex_ready", b + 1)
                link(nc.vector.tensor_reduce(red[:], ex[:], AX_X, ALU.add))
                link(nc.vector.reciprocal(red[:], red[:]))
                link(nc.vector.tensor_tensor(pr[:], ex[:], bc(red), ALU.mult))

                def pick(src, hot):
                    link(nc.vector.tensor_reduce(red[:], src[:], AX_X, ALU.max))
                    link(nc.vector.tensor_tensor(hot, src[:], bc(red), ALU.is_equal))
                    link(nc.vector.tensor_tensor(tmp8[:], hot, rankw, ALU.mult))
                    link(nc.vector.tensor_reduce(red[:], tmp8[:], AX_X, ALU.max))
                    link(nc.vector.tensor_tensor(hot, tmp8[:], bc(red), ALU.is_equal))

                pick(pr, oh[:, 0])
                link(nc.vector.scalar_tensor_tensor(pr2[:], oh[:, 0], -2.0, pr[:], ALU.mult, ALU.add))
                pick(pr2, oh[:, 1])
                link(nc.vector.tensor_tensor(ohs[:], oh[:, 0], oh[:, 1], ALU.add))
                after(dve, "rank_psum", b)
                nc.vector.tensor_copy(oh16[:], ohs[:]).then_inc(s["oh_ready"], 1)
                nc.vector.tensor_tensor(yall[:, subtiles(b), W_AT:W_AT + E], ohs[:], pr[:], ALU.mult).then_inc(s["w_kept"], 1)
                link(nc.vector.tensor_reduce(msum[:], ohs[:].rearrange("p j e -> p e j"), AX_X, ALU.add))
                link(nc.vector.tensor_tensor(macc[:], macc[:], msum[:], ALU.add))

            def place(b, par):
                link = chain(b * RT_STEPS + 18)
                after(dve, "rank_psum", b + 1)
                ranks = GW[:, 0:SUB * E].rearrange("p (j e) -> p j e", j=SUB)
                nc.vector.tensor_tensor(rk[:], ranks, reg0, ALU.add).then_inc(s["rk_read"], 1)
                link(nc.vector.tensor_copy(macc16[:], macc[:]))
                after(dve, "rk_read", b + 1)
                link(nc.vector.tensor_tensor(tmp16[:], oh[:], rk[:].unsqueeze(1).to_broadcast([P, TOP_K, SUB, E]), ALU.mult))
                link(nc.vector.tensor_reduce(slot_f[:], tmp16[:], AX_X, ALU.add))
                if not isinstance(b, int) or b > 1:
                    after(dve, f"scat{par}", (b - par) * (SUB * TOP_K * 8), alone=True)
                nc.vector.tensor_copy(slots[par][:], slot_f[:]).then_inc(s["slots_ready"], 1)

            def step(i, par):
                b, c, d, o = i, i - 1, i - 2, 1 - par
                if has_ln(i - 1):
                    after(dve, "ln_rs", i + 2)
                    after(dve, "xn_ready", all_of(i))
                    after(dve, "yn_ready", i - 4)
                    nc.vector.scalar_tensor_tensor(nb[o][:], mv[o][:, :, 0], -1.0, rs[o][:], ALU.mult,
                                                   ALU.mult).then_inc(s["nb_ready"], 1)
                if on(i, 5):
                    place(i - 5, o)
                if on(i, 1):
                    after(dve, "vs_psum", c + 1)
                    after(dve, "num_psum", c)
                    nc.vector.tensor_tensor(kvbd[:, 0:D], KV[:, 0:D], hmask[:, 0:D], ALU.mult)
                    nc.vector.tensor_scalar(kvbd[:, D:ND], hmask[:, D:ND], KV[:, D:D + 1], None,
                                            ALU.mult).then_inc(s["ks_masked"], 1)
                if on(i, 0):
                    after(dve, "q_psum", b + 1)
                    after(dve, "q_rot", b)
                    nc.vector.tensor_tensor(q_c[:], qp[:, 0:512], cosT, ALU.mult).then_inc(s["q_cos"], 1)
                    after(dve, "qp_psum", b + 1)
                    nc.vector.tensor_tensor(q_s[:], qp[:, 512:1024], sinT, ALU.mult).then_inc(s["q_sin"], 1)
                if on(i, 2):
                    after(dve, "wo_psum", d + 1)
                    after(dve, f"xre_full{par}", (d - par) * 8 + 16)
                    after(dve, "yn_ready", d - 1)
                    if not isinstance(i, int) or d > 1:
                        after(dve, f"x2_out{par}", (d - par) * 8)
                    nc.vector.tensor_tensor(x2[par][:], GW[:].rearrange("p (j d) -> p j d", j=SUB), xre[par][:],
                                            ALU.add).then_inc(s["x2_ready"], 1)
                if on(i, -2):
                    after(dve, f"xin_full{par}", (i + 2 - par) * 8 + 16, alone=True)
                if has_ln(i):
                    after(dve, "mv_ready", i + 2, alone=True)
                if on(i, 2):
                    after(dve, "x2_ready", d + 1, alone=True)
                    last = stats(x2[par], SUB)
                if on(i, -2):
                    last = stats(xin[par], 0)
                if has_ln(i):
                    last.then_inc(s["stats"], 1)
                if on(i, 0):
                    after(dve, "kvp_psum", b + 1)
                    after(dve, "ktok_ready", b)
                    k = kvp[:].rearrange("p (j c) -> p j c", j=SUB)[:, :, 0:D]
                    nc.vector.tensor_tensor(k_c[:], k, tabk[:, 0], ALU.mult)

                    def halves(v, t):
                        return v.rearrange("p j (h t e) -> p j h t e", h=H, t=2)[:, :, :, t, :]
                    for t in range(2):
                        last_k = nc.vector.tensor_tensor(halves(k_s[:], t), halves(k, 1 - t), halves(tabk[:, 1], t), ALU.mult)
                    last_k.then_inc(s["k_sin"], 1)
                if has_ln(i):
                    after(dve, "stats", i + 3, alone=True)
                    after(dve, "nb_ready", i + 1, alone=True)
                    for at, lag in ((0, -2), (SUB, 2)):
                        if on(i, lag):
                            for j in range(SUB):
                                last = nc.vector.bn_aggr(mv[par][:, at + j, :], st[:, at + j, :])
                    last.then_inc(s["mv_ready"], 1)
                    after(dve, "mv_ready", i + 3)
                    after(dve, "ln_rs", i + 2)
                    nc.vector.tensor_scalar(ve[:], mv[par][:, :, 1], EPS, None, ALU.add).then_inc(s["ve_ready"], 1)
                if on(i, 4):
                    shift_logits(i - 4)
                if on(i, 1):
                    after(dve, "num_psum", c + 1)
                    v = qp[:].rearrange("p (n m) -> p n m", n=2)[:, :, 0:2 * ND].rearrange("p n (j m) -> p n j m", j=2)
                    nc.vector.reciprocal(rden[:].rearrange("p (n j) h -> p n j h", n=2), v[:, :, :, D:ND]
                                         ).then_inc(s["rden_ready"], 1)
                    after(dve, "rden_ready", c + 1)
                    after(dve, "a_tr", c)
                    for n in range(2):
                        last = nc.vector.tensor_tensor(
                            att[:, 2 * n:2 * n + 2, :].rearrange("p j (h e) -> p j h e", h=H),
                            v[:, n, :, 0:D].rearrange("p j (h e) -> p j h e", h=H),
                            rden[:, 2 * n:2 * n + 2, :].unsqueeze(3).to_broadcast([P, 2, H, DK]), ALU.mult)
                    last.then_inc(s["att_ready"], 1)
                if on(i, 4):
                    choose(i - 4)
                if on(i, 1):
                    after(dve, "a_tr", c + 1)
                    after(dve, "wo_psum", c)
                    nc.vector.scalar_tensor_tensor(oT[:], CV[:], lb, gT[o][:], ALU.add,
                                                   ALU.mult).then_inc(s["o_ready"], 1)
                if on(i, -1):
                    after(dve, "xnTh_ready", i + 2)
                    after(dve, "a_tr", i)
                    nc.vector.tensor_tensor(xnT_l[o][:, PAD:PAD + S], XB[:], xnT_h[o][:, PAD:PAD + S].bitcast(F32),
                                            ALU.subtract).then_inc(s["xnTl_ready"], 1)

            dve.wait_ge(s["first_in"], 16)
            nc.vector.tensor_copy(wproj_h[:], wproj).then_inc(s["wsplit"], 1)
            dve.wait_ge(s["second_in"], 16)
            nc.vector.tensor_tensor(wconv[:], lrows, wproj[:, 4:5, :].to_broadcast([P, TAPS, D]),
                                    ALU.mult).then_inc(s["wsplit"], 1)
            nc.vector.tensor_copy(bef16[:], bef).then_inc(s["bef_set"], 1)
            nc.vector.tensor_copy(yall[:, :, ID_AT], ids)
            dve.wait_ge(s["wsplit"], 2)
            nc.vector.tensor_tensor(wproj_l[:], wproj, wproj_h[:].bitcast(F32), ALU.subtract).then_inc(s["wsplit"], 1)
            nc.vector.tensor_copy(wconv_h[:], wconv[:]).then_inc(s["wsplit"], 1)
            dve.wait_ge(s["wsplit"], 4)
            nc.vector.tensor_tensor(wconv_l[:], wconv[:], wconv_h[:].bitcast(F32), ALU.subtract).then_inc(s["wsplit"], 1)
            dve.wait_ge(s["tabk_in"], 16)
            pipeline(dve, step)

            tb = [0]

            def link(ins):
                tb[0] += 1
                ins.then_inc(s["tb"], 1)
                dve.wait_ge(s["tb"], tb[0])

            def row(ap, n, m):
                return ap[0:1, :].unsqueeze(1).to_broadcast([1, n, m])

            nk = N_COUNT
            dve.wait_ge(s["cnt_psum"], 1)
            dve.wait_ge(s["rowc_in"], 16)
            link(nc.vector.tensor_copy(cnt[:], GW[0:1, 0:E]))
            nc.vector.tensor_tensor(fill_at[:], cnt[:], reg0[0:1, 0, :], ALU.add).then_inc(s["fill_ready"], 1)
            link(nc.vector.tensor_tensor(gt[:], thr, cnt[:].unsqueeze(2).to_broadcast([1, E, nk]), ALU.is_lt))
            link(nc.vector.tensor_reduce(ntile[:], gt[:], AX_X, ALU.add))
            link(nc.vector.tensor_tensor(cm[:], cumu, row(ntile, E, E), ALU.mult))
            link(nc.vector.tensor_reduce(incl[:], cm[:], AX_X, ALU.add))
            link(nc.vector.tensor_scalar(skip[:], ntile[:], -float(TS), float(CAP), ALU.mult, ALU.add))
            link(nc.vector.tensor_tensor(passed[:], row(incl, N_TILES, E), tno, ALU.is_le))
            link(nc.vector.tensor_tensor(pskip[:], passed[:], row(skip, N_TILES, E), ALU.mult))
            link(nc.vector.tensor_reduce(trow_f[:], pskip[:], AX_X, ALU.add))
            link(nc.vector.scalar_tensor_tensor(trow_f[:], tno[:, :, 0], float(TS), trow_f[:], ALU.mult, ALU.add))
            nc.vector.tensor_scalar(trow[:], trow_f[:], float(E * CAP), None, ALU.min).then_inc(s["table_ready"], 1)
            link(nc.vector.tensor_reduce(texp_f[:], passed[:], AX_X, ALU.add))
            nc.vector.tensor_scalar(texp[:], texp_f[:], float(E - 1), None, ALU.min).then_inc(s["table_ready"], 1)

            def x_low(t):
                after(dve, "xTh_ready", t.no + 1)
                nc.vector.tensor_tensor(xT_l[t.buf][:], XB[:], xT_h[t.buf][:].bitcast(F32),
                                        ALU.subtract).then_inc(s["xTl_ready"], 1)

            def weights(t):
                after(dve, f"bst_in{t.buf}", t.fills * 16)
                after(dve, f"xg_in{t.buf}", t.fills * 16)
                nc.vector.tensor_tensor(wsel[:], xg[t.buf][:, :, W_AT:W_AT + E],
                                        bst[t.buf][:, FC + 1:BPACK].unsqueeze(1).to_broadcast([P, TSUB, E]),
                                        ALU.mult).then_inc(s["wsel_ready"], 1)
                after(dve, "yo_ready", t.no - 2)
                nc.vector.tensor_copy(tok_f[t.buf][:], xg[t.buf][:, :, ID_AT])
                after(dve, "wsel_ready", t.no + 1)
                nc.vector.tensor_reduce(wv[t.buf][:], wsel[:], AX_X, ALU.add).then_inc(s["wv_ready"], 1)

            def weigh(t):
                after(dve, "wv_ready", t.no + 1)
                after(dve, "acc_done", (t.no - 2) * (TSUB * 16))
                nc.vector.tensor_copy(tok[t.buf][:], tok_f[t.buf][:])
                after(dve, "yo_tr", t.no + 1)
                nc.vector.tensor_tensor(yo[t.buf][:], TY[:].rearrange("p (j d) -> p j d", j=TSUB),
                                        wv[t.buf][:].unsqueeze(2).to_broadcast([P, TSUB, D]), ALU.mult).then_inc(s["yo_ready"], 1)

            def tile_step(t):
                before, behind = t.at(-1), t.at(1)
                for c in range(FC):
                    if t.real:
                        n = t.no * FC + c
                        after(dve, "h_silu", n + 1)
                        after(dve, "h_psum", n)
                        nc.vector.tensor_copy(hh[c][:], hf[c][:]).then_inc(s["h_high"], 1)
                        after(dve, "h_high", n + 1)
                        nc.vector.tensor_tensor(hl[c][:], hf[c][:], hh[c][:].bitcast(F32), ALU.subtract).then_inc(s["h_low"], 1)
                    if c == 1 and behind.real:
                        x_low(behind)
                        weights(behind)
                if before.real:
                    weigh(before)

            x_low(Tile(0, 0))
            weights(Tile(0, 0))
            tile_pipeline(dve, tile_step, 1)


RT_STEPS = 21
_INS = ["x", "first", "second", "tables_k", "tail_rows", "row_consts", "w_experts", "b_experts"]


def rope_tables():
    inv = (np.float32(1.0) / np.float32(10000.0) ** (np.arange(0, DK, 2, dtype=np.float32) / np.float32(DK))).astype(np.float32)
    freqs = np.arange(S, dtype=np.float32)[:, None] * inv[None, :]
    emb = np.concatenate([freqs, freqs], axis=1)
    sign = np.where(np.arange(DK) < DK // 2, -1.0, 1.0).astype(np.float32)
    cos = np.tile(np.cos(emb).astype(np.float32), (1, H))
    sin = np.tile(np.sin(emb).astype(np.float32) * sign[None, :], (1, H))
    return cos, sin


def head_masks():
    head = np.arange(D) // DK
    full = (head[:, None] == head[None, :]).astype(np.float32)
    each = (head[:, None] == np.arange(H)[None, :]).astype(np.float32)
    return np.concatenate([full, each], axis=1) * np.float32(DK ** -0.5)


def constants():
    cos, sin = rope_tables()
    f = np.float32
    tail = np.zeros((TS, ROW), f)
    tail[:, ID_AT] = N_TOK + np.arange(TS)
    experts = np.arange(E, dtype=f)
    thresholds = np.broadcast_to(np.arange(0, N_TOK, TS, dtype=f), (E, N_COUNT))
    tile_no = np.broadcast_to(np.arange(N_TILES, dtype=f)[:, None], (N_TILES, E))
    return {
        "cos_t": cos.T, "sin_t": sin.T, "head_mask": head_masks(), "ident": np.eye(P, dtype=f),
        "tables_k": np.stack([cos, sin]).reshape(2, SUB, P, D).transpose(2, 0, 1, 3),
        "rank_w": np.tile(E - experts, (P, SUB)),
        "region": np.tile(experts * CAP, (P, SUB)),
        "before": np.triu(np.ones((P, P), f), 1),
        "ids": np.arange(N_TOK, dtype=f).reshape(NB * SUB, P).T,
        "tail_rows": tail.reshape(P, TSUB, ROW),
        "row_consts": np.concatenate([thresholds.reshape(-1), np.tril(np.ones((E, E), f)).reshape(-1), tile_no.reshape(-1)])[None],
    }


def kernel(**inputs):
    import concourse.bacc as _bacc
    from concourse.bass_utils import run_bass_kernel_spmd as _run

    g = {n: np.asarray(v) for n, v in inputs.items()}
    rot = np.arange(D).reshape(H, 2, DK // 2)[:, ::-1].reshape(-1)
    wq, wk, wv, wg = (g[f"L0_attn_{n}"] for n in ("Wq", "Wk", "Wv", "Wg"))
    w1, w2 = g["L0_ffn_w1"], g["L0_ffn_w2"]
    b1 = g["L0_ffn_b1"].reshape(E, FC, P).transpose(2, 0, 1)
    b2 = g["L0_ffn_b2"].T[:, :, None]
    code = np.broadcast_to(np.eye(E, dtype=b1.dtype), (P, E, E))
    lay = {
        **constants(),
        "x": g["L0_attn_hidden_states"].reshape(N_TOK, D),
        "w_proj": np.concatenate([wq.T, wq[rot].T, wg.T, wk.T, wv.T], axis=1),
        "w_o": g["L0_attn_Wo"].T,
        "lepe_rows": np.broadcast_to(g["L0_attn_lepe_w"].reshape(D, TAPS).T.reshape(-1), (P, TAPS * D)),
        "lepe_b": g["L0_attn_lepe_b"].reshape(D, 1),
        "gate_t": g["L0_ffn_gate_w"].T,
        "w_experts": np.concatenate([w1, w2.reshape(E, FC, P, D).transpose(0, 2, 1, 3).reshape(E, P, FC * D)], axis=2),
        "b_experts": np.concatenate([b1, b2, code], axis=2),
    }
    lay["first"] = np.concatenate([lay[n] for n in FIRST], axis=1)
    lay["second"] = np.concatenate([lay[n] for n in SECOND], axis=1)
    nc = _bacc.Bacc("TRN2", target_bir_lowering=False, num_devices=1)
    arrays, args = {}, []
    for name in _INS:
        a = np.ascontiguousarray(lay[name])
        arrays[f"in_{name}"] = a
        args.append(nc.dram_tensor(f"in_{name}", a.shape, mybir.dt.from_np(a.dtype), kind="ExternalInput").ap())
    args.append(nc.dram_tensor("out_x", (N_TOK + TS, D), F32, kind="ExternalOutput").ap())
    build(nc, *args)
    r = _run(nc, [arrays], core_ids=[0])
    return r.results[0]["out_x"][:N_TOK].reshape(NB, S, D)
```

```python
from contextlib import ExitStack

import numpy as np
import concourse.bass as bass
from concourse import mybir

ALU = mybir.AluOpType
ACT = mybir.ActivationFunctionType
F32 = mybir.dt.float32
F32R = mybir.dt.float32r
BF16 = mybir.dt.bfloat16
U32 = mybir.dt.uint32
AX_X = mybir.AxisListType.X

P = 128
NB = 16
S = 512
SUB = S // P
N_TOK = NB * S
D = 128
H = 8
DK = D // H
TAPS = 5
PAD = TAPS // 2
E = 8
TOP_K = 2
F = 512
FC = F // P
EPS = 1e-5
ND = D + H

TS = 512
TSUB = TS // P
CAP = N_TOK + TS
N_TILES = (TOP_K * N_TOK + E * (TS - 1)) // TS
W_AT, ID_AT = D, D + E
ROW = D + E + 1
WPACK = 2 * F
BPACK = FC + 1 + E
NBUF = 3
DOWN_LAG = 2
N_COUNT = N_TOK // TS

LEAD, LAG = 2, 5
LOOP_FROM, LOOP_TO = 6, 11
OWN_ROWS = 7

N_PROJ = 5
FIRST = {"w_proj": N_PROJ * D, "ident": P}
SECOND = {"lepe_rows": TAPS * D, "cos_t": S, "sin_t": S, "head_mask": ND, "w_o": D, "lepe_b": 1, "gate_t": E,
          "rank_w": SUB * E, "region": SUB * E, "before": P, "ids": NB * SUB}


def build(nc, x, first, second, tables_k, tail_rows, row_consts, w_experts, b_experts, out):
    rows_in = nc.dram_tensor("rows_in", (E * CAP + TS, ROW), F32, kind="Internal").ap()

    with ExitStack() as ctx:
        def sb(name, shape, dt=F32):
            return ctx.enter_context(nc.sbuf_tensor(name, shape, dt))

        def bank(name, n=1):
            return ctx.enter_context(nc.psum_tensor(name, [P, n * 512], F32))

        def sem(name):
            return ctx.enter_context(nc.semaphore(name))

        first_sb = sb("first_sb", [P, sum(FIRST.values())])
        second_sb = sb("second_sb", [P, sum(SECOND.values())])

        def part(whole, widths, name):
            names = list(widths)
            at = sum(widths[n] for n in names[:names.index(name)])
            return whole[:, at:at + widths[name]]

        wproj = part(first_sb, FIRST, "w_proj").rearrange("p (n d) -> p n d", n=N_PROJ)
        idn = part(first_sb, FIRST, "ident")
        lrows = part(second_sb, SECOND, "lepe_rows").rearrange("p (t d) -> p t d", t=TAPS)
        cosT = part(second_sb, SECOND, "cos_t")
        sinT = part(second_sb, SECOND, "sin_t")
        hmask = part(second_sb, SECOND, "head_mask")
        wo = part(second_sb, SECOND, "w_o")
        lb = part(second_sb, SECOND, "lepe_b")
        gateT = part(second_sb, SECOND, "gate_t")
        rankw = part(second_sb, SECOND, "rank_w").rearrange("p (j e) -> p j e", j=SUB)
        reg0 = part(second_sb, SECOND, "region").rearrange("p (j e) -> p j e", j=SUB)
        bef = part(second_sb, SECOND, "before")
        ids = part(second_sb, SECOND, "ids")
        wproj_h = sb("wproj_h", [P, N_PROJ, D], F32R)
        wproj_l = sb("wproj_l", [P, N_PROJ, D], F32R)
        wconv = sb("wconv", [P, TAPS, D])
        wconv_h = sb("wconv_h", [P, TAPS, D], F32R)
        wconv_l = sb("wconv_l", [P, TAPS, D], F32R)
        bef16 = sb("bef16", [P, P], BF16)
        one16 = sb("one16", [P, P], BF16)
        half = sb("half", [P, 2 * SUB])
        ones_row = sb("ones_row", [1, P])
        table_load = sb("table_load", [1, 1])
        consts_row = sb("consts_row", [1, E * N_COUNT + E * E + N_TILES * E])
        thr = consts_row[:, 0:E * N_COUNT].rearrange("p (e n) -> p e n", e=E)
        cumu = consts_row[:, E * N_COUNT:E * N_COUNT + E * E].rearrange("p (e f) -> p e f", e=E)
        tno = consts_row[:, E * N_COUNT + E * E:].rearrange("p (t e) -> p t e", e=E)
        tail = sb("tail", [P, TSUB, ROW])

        wres = sb("wres", [P, E, 2, WPACK], F32R)
        bres = sb("bres", [P, E, BPACK])

        st = sb("st", [P, 2 * SUB, 6])
        mv = [sb(f"mv{i}", [P, 2 * SUB, 2]) for i in range(2)]
        ve = sb("ve", [P, 2 * SUB])
        rs = [sb(f"rs{i}", [P, 2 * SUB]) for i in range(2)]
        nb = [sb(f"nb{i}", [P, 2 * SUB]) for i in range(2)]

        lgs = sb("lgs", [P, SUB, E])
        lg = sb("lg", [P, SUB, E])
        ex = sb("ex", [P, SUB, E])
        pr = sb("pr", [P, SUB, E])
        pr2 = sb("pr2", [P, SUB, E])
        oh = sb("oh", [P, TOP_K, SUB, E])
        ohs = sb("ohs", [P, SUB, E])
        oh16 = sb("oh16", [P, SUB, E], BF16)
        tmp8 = sb("tmp8", [P, SUB, E])
        tmp16 = sb("tmp16", [P, TOP_K, SUB, E])
        red = sb("red", [P, SUB])
        msum = sb("msum", [P, E])
        macc = sb("macc", [P, E])
        macc16 = sb("macc16", [P, E], BF16)
        rk = sb("rk", [P, SUB, E])
        slot_f = sb("slot_f", [P, TOP_K, SUB])
        slots = [sb(f"slots{i}", [P, TOP_K, SUB], U32) for i in range(2)]

        cnt = sb("cnt", [1, E])
        fill_at = sb("fill_at", [1, E], U32)
        gt = sb("gt", [1, E, N_COUNT])
        ntile = sb("ntile", [1, E])
        cm = sb("cm", [1, E, E])
        incl = sb("incl", [1, E])
        skip = sb("skip", [1, E])
        passed = sb("passed", [1, N_TILES, E])
        pskip = sb("pskip", [1, N_TILES, E])
        trow_f = sb("trow_f", [1, N_TILES])
        texp_f = sb("texp_f", [1, N_TILES])
        trow = sb("trow", [1, N_TILES], U32)
        texp = sb("texp", [1, N_TILES], U32)

        attention = ExitStack()

        def sa(name, shape, dt=F32):
            return attention.enter_context(nc.sbuf_tensor(name, shape, dt))

        wraw = [sa(f"wraw{i}", [P, WPACK]) for i in range(2)]
        xin = [sa(f"xin{i}", [P, SUB, D]) for i in range(2)]
        xre = [sa(f"xre{i}", [P, SUB, D]) for i in range(2)]
        xn = sa("xn", [P, SUB, D])
        xnT_h = [sa(f"xnT_h{i}", [P, S + 2 * PAD], F32R) for i in range(2)]
        xnT_l = [sa(f"xnT_l{i}", [P, S + 2 * PAD], F32R) for i in range(2)]
        tabk = sa("tabk", [P, 2, SUB, D])
        q_c = sa("q_c", [P, S])
        q_s = sa("q_s", [P, S])
        k_c = sa("k_c", [P, SUB, D])
        k_s = sa("k_s", [P, SUB, D])
        qrot = [sa(f"qrot{i}", [P, S]) for i in range(2)]
        ktok = sa("ktok", [P, SUB, D])
        vtok = sa("vtok", [P, SUB, D + 1])
        gT = [sa(f"gT{i}", [P, S]) for i in range(2)]
        xsum = [sa(f"xsum{i}", [P, 1]) for i in range(2)]
        vrow = sa("vrow", [1, ND])
        kvbd = sa("kvbd", [P, ND])
        rden = sa("rden", [P, SUB, H])
        att = sa("att", [P, SUB, D])
        oT = sa("oT", [P, S])
        x2 = [sa(f"x2{i}", [P, SUB, D]) for i in range(2)]
        yT = sa("yT", [P, S])
        yrow = [sa(f"yrow{i}", [P, SUB, ROW]) for i in range(2 + OWN_ROWS)]

        def rows_of(b, par):
            return yrow[2 + b - (NB - OWN_ROWS)] if isinstance(b, int) and b >= NB - OWN_ROWS else yrow[par]

        def shares_rows(b):
            return not isinstance(b, int) or 1 < b < NB - OWN_ROWS

        attention.close()

        xg = [sb(f"xg{i}", [P, TSUB, ROW]) for i in range(NBUF)]
        wst = [sb(f"wst{i}", [P, 2, WPACK], F32R) for i in range(NBUF)]
        bst = [sb(f"bst{i}", [P, BPACK]) for i in range(NBUF)]
        xT_h = [sb(f"xT_h{i}", [P, TS], F32R) for i in range(NBUF)]
        xT_l = [sb(f"xT_l{i}", [P, TS], F32R) for i in range(NBUF)]
        wsel = sb("wsel", [P, TSUB, E])
        wv = [sb(f"wv{i}", [P, TSUB]) for i in range(NBUF)]
        tok_f = [sb(f"tok_f{i}", [P, TSUB]) for i in range(NBUF)]
        tok = [sb(f"tok{i}", [P, TSUB], U32) for i in range(NBUF)]
        hf = [sb(f"hf{i}", [P, TS]) for i in range(FC)]
        hh = [sb(f"hh{i}", [P, TS], F32R) for i in range(FC)]
        hl = [sb(f"hl{i}", [P, TS], F32R) for i in range(FC)]
        yTs = sb("yTs", [P, TS])
        yo = [sb(f"yo{i}", [P, TSUB, D]) for i in range(NBUF)]

        qp = bank("qp", 2)
        kvp = bank("kvp", 2)
        KV, CV, GW, XB = [bank(n) for n in ("kv", "conv", "gate_wo", "rows")]
        HB, YB, TY = [qp[:, 0:512], qp[:, 512:1024], kvp[:, 0:512]], [kvp[:, 512:1024], KV, CV], GW

        names = """first_in second_in tabk_in tail_in rowc_in wraw_in0 wraw_in1 bres_in xin_full0 xin_full1 xre_full0 xre_full1
            consts_set ones_set wsplit w_high w_low bef_set
            st1_ready st2_ready mv1_ready mv2_ready ve_ready ln_rs nb_ready xn_ready xnT_psum xnTh_ready xnTl_ready
            q_psum qp_psum q_sin q_rot kvp_psum k_sin ktok_ready vtok_ready conv_psum g_psum g_saved
            kv_psum vs_psum v_row ks_masked num_psum rden_ready att_ready a_tr o_ready
            wo_psum x2_ready x2_out0 x2_out1 yn_ready w_kept id_kept y_tr yT_ready gate_psum lgs_ready
            lg_sub ex_ready rt oh_ready rank_psum rk_read slots_ready scat0 scat1 cnt_psum fill_ready tb table_ready
            tails_in dummy_in out_dummy
            xg_in0 xg_in1 xg_in2 wst_in0 wst_in1 wst_in2 bst_in0 bst_in1 bst_in2 x_tr xTh_ready xTl_ready wsel_ready wv_ready
            h_psum h_silu h_high h_low y_psum yT_saved yo_tr yo_ready acc_done""".split()
        s = {n: sem(n) for n in names}

        def after(eng, name, n, alone=False):
            if isinstance(n, int) and n <= 0:
                return
            eng.wait_ge(s[name], n)
            if alone:
                eng.nop(nofuse=True)

        block = ctx.enter_context(nc.Block())

        def hbank(t, c):
            return HB[(t.buf * FC + c) % len(HB)]

        def has_ln(i):
            return on(i, -2) or on(i, 2)

        def pipeline(eng, step):
            for i in range(-LEAD, LOOP_FROM):
                step(i, i % 2)
            with eng.Fori(LOOP_FROM, LOOP_TO, 2) as i:
                step(i, 0)
                step(i + 1, 1)
            for i in range(LOOP_TO + 1, NB + LAG):
                step(i, i % 2)

        def on(i, lag):
            return not isinstance(i, int) or 0 <= i - lag < NB

        def all_of(n):
            return min(n, NB) if isinstance(n, int) else n

        class Tile:
            def __init__(self, g, k):
                self.no, self.buf, self.fills = g * NBUF + k, k, g + 1
                self.at = lambda d: Tile(g + (k + d) // NBUF, (k + d) % NBUF)
                self.real = not isinstance(g, int) or 0 <= self.no < N_TILES

        def tile_pipeline(eng, step, extra):
            rounds = N_TILES // NBUF
            assert rounds * NBUF == N_TILES
            for i in range(2 * NBUF):
                step(Tile(i // NBUF, i % NBUF))
            with eng.Fori(2, rounds - 1) as g:
                for k in range(NBUF):
                    step(Tile(g, k))
            for i in range((rounds - 1) * NBUF, N_TILES + extra):
                step(Tile(i // NBUF, i % NBUF))

        xv = x.rearrange("(b j p) d -> p (b j) d", p=P, j=SUB)
        ov = out[0:N_TOK, :].rearrange("(b j p) d -> p (b j) d", p=P, j=SUB)

        def subtiles(b):
            return slice(b * SUB, (b + 1) * SUB) if isinstance(b, int) else bass.ds(b * SUB, SUB)

        def batch(v, b):
            return v[:, subtiles(b), :]

        @block.sync
        def _(sp):
            sp.dma_start(xin[0][:], batch(xv, 0)).then_inc(s["xin_full0"], 16)
            sp.dma_start(first_sb[:], first).then_inc(s["first_in"], 16)
            sp.dma_start(xin[1][:], batch(xv, 1)).then_inc(s["xin_full1"], 16)
            sp.dma_start(second_sb[:], second).then_inc(s["second_in"], 16)
            sp.dma_start(tabk[:], tables_k).then_inc(s["tabk_in"], 16)
            sp.dma_start(tail[:], tail_rows).then_inc(s["tail_in"], 16)
            sp.dma_start(consts_row[:], row_consts).then_inc(s["rowc_in"], 16)
            sp.dma_start(bres[:], b_experts).then_inc(s["bres_in"], 16)

            def load_expert(e):
                after(sp, "w_low", e - 1)
                sp.dma_start(wraw[e % 2][:], w_experts[e]).then_inc(s[f"wraw_in{e % 2}"], 16)

            load_expert(0)
            load_expert(1)
            sp.wait_ge(s["tail_in"], 16)
            sp.dma_start(rows_in[E * CAP:E * CAP + TS, :].rearrange("(p j) w -> p j w", p=P), tail[:]).then_inc(s["dummy_in"], 16)
            sp.dma_start(out[N_TOK:N_TOK + TS, :].rearrange("(p j) d -> p j d", p=P), tail[:, :, 0:D]).then_inc(s["out_dummy"], 16)

            def step(i, par):
                if on(i, 1):
                    after(sp, "x2_ready", i - 2)
                    sp.dma_start(xre[1 - par][:], batch(xv, i - 1)).then_inc(s[f"xre_full{1 - par}"], 16)
                if on(i, -3) and (not isinstance(i, int) or i > -2):
                    after(sp, "xn_ready", i + 2)
                    sp.dma_start(xin[1 - par][:], batch(xv, i + 3)).then_inc(s[f"xin_full{1 - par}"], 16)
                if isinstance(i, int) and 0 <= i < E // 2 - 1:
                    load_expert(2 * i + 2)
                    load_expert(2 * i + 3)
                if on(i, 2):
                    after(sp, "x2_ready", i - 1)
                    sp.dma_start(batch(ov, i - 2), x2[par][:]).then_inc(s[f"x2_out{par}"], 16)

            pipeline(sp, step)

            sp.wait_ge(s["fill_ready"], 1)
            for e in range(E):
                r = sp.value_load(fill_at[0:1, e:e + 1], min_val=e * CAP, max_val=e * CAP + N_TOK)
                sp.dma_start(rows_in[bass.ds(r, TS), :].rearrange("(p j) w -> p j w", p=P), tail[:]).then_inc(s["tails_in"], 16)
            sp.wait_ge(s["table_ready"], 2)
            sp.wait_ge(s["w_low"], E)
            sp.wait_ge(s["bres_in"], 16)

            def at(t):
                return slice(t.no, t.no + 1) if isinstance(t.no, int) else bass.ds(t.no, 1)

            def load_rows(t):
                r = sp.value_load(trow[0:1, at(t)], min_val=0, max_val=E * CAP)
                after(sp, "x_tr", t.no - 2)
                after(sp, "wv_ready", t.no - 2)
                sp.dma_start(xg[t.buf][:], rows_in[bass.ds(r, TS), :].rearrange("(p j) w -> p j w", p=P)
                             ).then_inc(s[f"xg_in{t.buf}"], 16)

            def load_weights(t):
                e = sp.value_load(texp[0:1, at(t)], min_val=0, max_val=E - 1)
                after(sp, "y_psum", t.no - 2)
                sp.dma_start(wst[t.buf][:].bitcast(F32),
                             wres[:, bass.ds(e, 1), :, :].rearrange("p a t w -> p (a t) w").bitcast(F32)
                             ).then_inc(s[f"wst_in{t.buf}"], 16)
                after(sp, "yT_saved", t.no - 2)
                sp.dma_start(bst[t.buf][:], bres[:, bass.ds(e, 1), :].rearrange("p a w -> p (a w)")
                             ).then_inc(s[f"bst_in{t.buf}"], 16)

            def load_tile(t):
                if isinstance(t.no, int) and t.no == 0:
                    load_weights(t)
                    sp.wait_ge(s["tails_in"], E * 16)
                    sp.wait_ge(s["dummy_in"], 16)
                    sp.wait_ge(s["scat0"], NB // 2 * SUB * TOP_K * 16)
                    sp.wait_ge(s["scat1"], NB // 2 * SUB * TOP_K * 16)
                    load_rows(t)
                if t.at(1).real:
                    load_rows(t.at(1))
                if not isinstance(t.no, int) or t.no > 0:
                    load_weights(t)

            tile_pipeline(sp, load_tile, 0)
            sp.wait_ge(s["acc_done"], N_TILES * TSUB * 16)

        @block.tensor
        def _(pe):
            def transposes(dst, src, name):
                for j in range(SUB):
                    last = nc.tensor.transpose(dst[:, j * P:(j + 1) * P], src(j), idn)
                last.then_inc(s[name], 1)

            def product(dst, w_h, w_l, r_h, r_l, first, last, done=None):
                nc.tensor.matmul(dst, w_h, r_h, start=first, stop=False)
                nc.tensor.matmul(dst, w_l, r_h, start=False, stop=False)
                third = nc.tensor.matmul(dst, w_h, r_l, start=False, stop=last)
                if done:
                    third.then_inc(s[done], 1)
                return third

            def project(dst, n, par, name):
                product(dst, wproj_h[:, n, :], wproj_l[:, n, :], xnT_h[par][:, PAD:PAD + S], xnT_l[par][:, PAD:PAD + S],
                        True, True).then_inc(s[name], 1)

            pe.wait_ge(s["first_in"], 16)
            pe.wait_ge(s["ones_set"], 1)

            def step(i, par):
                b, c, o = i, i - 1, 1 - par
                if on(i, 1):
                    after(pe, "vtok_ready", c + 1)
                    nc.tensor.matmul(kvp[0:1, 0:D], xsum[o][:], wproj[:, 4, :], start=True, stop=True).then_inc(s["vs_psum"], 1)
                    after(pe, "ktok_ready", c + 1)
                    after(pe, "ks_masked", c)
                    for j in range(SUB):
                        last = nc.tensor.matmul(KV[:, 0:D + 1], ktok[:, j, :], vtok[:, j, :],
                                                start=(j == 0), stop=(j == SUB - 1))
                    last.then_inc(s["kv_psum"], 1)
                if on(i, 0):
                    after(pe, "xnTl_ready", b + 1)
                    after(pe, "att_ready", b - 1)
                    if isinstance(i, int) and i == 0:
                        pe.wait_ge(s["wsplit"], 2)
                    project(qp[:, 0:512], 0, par, "q_psum")
                    project(qp[:, 512:1024], 1, par, "qp_psum")
                if on(i, 4):
                    after(pe, "oh_ready", i - 3)
                    after(pe, "xnTl_ready", all_of(i + 1))
                    after(pe, "lgs_ready", all_of(i - 3))
                    for j in range(SUB):
                        dst = XB[:, j * E:(j + 1) * E]
                        nc.tensor.matmul(dst, bef16[:], oh16[:, j, :], start=True, stop=False)
                        for k in range(j):
                            nc.tensor.matmul(dst, one16[:], oh16[:, k, :], start=False, stop=False)
                        last = nc.tensor.matmul(dst, one16[:], macc16[:], start=False, stop=True)
                    last.then_inc(s["rank_psum"], 1)
                if on(i, 2):
                    after(pe, "o_ready", i - 1)
                    after(pe, "g_saved", all_of(i))
                    for j in range(SUB):
                        last = nc.tensor.matmul(GW[:, j * D:(j + 1) * D], oT[:, j * P:(j + 1) * P], wo,
                                                start=True, stop=True)
                    last.then_inc(s["wo_psum"], 1)
                if on(i, 1):
                    after(pe, "ks_masked", c + 1)
                    after(pe, "v_row", c + 1)
                    after(pe, "q_rot", c + 1)
                    if on(i, 0):
                        after(pe, "q_sin", b + 1)
                    for j in range(SUB):
                        at = j // 2 * 512 + j % 2 * ND
                        nc.tensor.matmul(qp[:, at:at + ND], qrot[o][:, j * P:(j + 1) * P], kvbd[:], start=True, stop=False)
                        last = nc.tensor.matmul(qp[:, at:at + ND], ones_row[:], vrow[:], start=False, stop=True)
                    last.then_inc(s["num_psum"], 1)
                if on(i, 3):
                    after(pe, "yn_ready", i - 2)
                    after(pe, "xnTl_ready", all_of(i + 1))
                    after(pe, "rk_read", i - 3)
                    transposes(XB, lambda j: rows_of(i - 3, o)[:, j, 0:D], "y_tr")
                if on(i, 0):
                    after(pe, "v_row", b)
                    for j in range(SUB):
                        rows = slice(PAD + j * P, PAD + (j + 1) * P)
                        dst = kvp[:, 2 * j * D:2 * (j + 1) * D]
                        nc.tensor.matmul(dst, xnT_h[par][:, rows], wproj_h[:, 3:5, :], start=True, stop=False)
                        nc.tensor.matmul(dst, xnT_h[par][:, rows], wproj_l[:, 3:5, :], start=False, stop=False)
                        last = nc.tensor.matmul(dst, xnT_l[par][:, rows], wproj_h[:, 3:5, :], start=False, stop=True)
                    last.then_inc(s["kvp_psum"], 1)
                if on(i, 3):
                    after(pe, "yT_ready", i - 2)
                    for j in range(SUB):
                        last = nc.tensor.matmul(XB[:, j * E:(j + 1) * E], yT[:, j * P:(j + 1) * P], gateT,
                                                start=True, stop=True)
                    last.then_inc(s["gate_psum"], 1)
                if on(i, 1):
                    after(pe, "att_ready", c + 1)
                    for j in range(SUB):
                        last = nc.tensor.matmul(CV[:, j * P:(j + 1) * P], att[:, j, :], idn, start=False, stop=True,
                                                skip_group_check=True)
                    last.then_inc(s["a_tr"], 1)
                if on(i, -1):
                    after(pe, "xn_ready", i + 2)
                    after(pe, "xnTl_ready", i + 1)
                    if on(i, 3):
                        after(pe, "lgs_ready", i - 2)
                    transposes(XB, lambda j: xn[:, j, :], "xnT_psum")
                if on(i, 0):
                    if on(i, 2):
                        after(pe, "x2_ready", i - 1)
                    project(GW[:], 2, par, "g_psum")
                if on(i, 0):
                    after(pe, "o_ready", b)
                    if isinstance(i, int) and i == 0:
                        pe.wait_ge(s["second_in"], 16)
                        pe.wait_ge(s["wsplit"], 5)
                        pe.wait_ge(s["bef_set"], 1)
                    for t in range(TAPS):
                        product(CV[:], wconv_h[:, t, :], wconv_l[:, t, :], xnT_h[par][:, t:t + S], xnT_l[par][:, t:t + S],
                                t == 0, t == TAPS - 1, "conv_psum" if t == TAPS - 1 else None)

            pipeline(pe, step)
            pe.wait_ge(s["slots_ready"], NB)
            nc.tensor.matmul(GW[:, 0:E], one16[:], macc16[:], start=True, stop=True).then_inc(s["cnt_psum"], 1)

            def rows_to_features(t):
                after(pe, f"xg_in{t.buf}", t.fills * 16)
                after(pe, "xTl_ready", t.no)
                transposes(XB, lambda j: xg[t.buf][:, j, 0:D], "x_tr")

            def up(t, c):
                n = t.no * FC + c
                if c == 0:
                    after(pe, f"wst_in{t.buf}", t.fills * 16)
                    after(pe, "xTl_ready", t.no + 1)
                after(pe, "h_silu", n - len(HB) + 1)
                product(hbank(t, c)[:], wst[t.buf][:, 0, c * P:(c + 1) * P], wst[t.buf][:, 1, c * P:(c + 1) * P],
                        xT_h[t.buf][:], xT_l[t.buf][:], True, True).then_inc(s["h_psum"], 1)

            def down(t, c):
                if c == 0:
                    after(pe, "yT_saved", t.no - NBUF + 1)
                after(pe, "h_low", t.no * FC + c + 1)
                m = product(YB[t.buf][:], wst[t.buf][:, 0, F + c * D:F + (c + 1) * D],
                            wst[t.buf][:, 1, F + c * D:F + (c + 1) * D], hh[c][:], hl[c][:], c == 0, c == FC - 1)
                if c == FC - 1:
                    m.then_inc(s["y_psum"], 1)

            def features_to_rows(t):
                after(pe, "yT_saved", t.no + 1)
                after(pe, "yo_ready", t.no)
                transposes(TY, lambda j: yTs[:, j * P:(j + 1) * P], "yo_tr")

            for name in ("att_ready", "k_sin", "vtok_ready", "ks_masked", "v_row", "o_ready", "xnTl_ready", "lgs_ready"):
                pe.wait_ge(s[name], NB)
            pe.wait_ge(s["fill_ready"], 1)
            rows_to_features(Tile(0, 0))

            def tile_step(t):
                before, behind = t.at(-1), t.at(1)
                for c in range(FC):
                    if t.real:
                        up(t, c)
                    if c < DOWN_LAG:
                        if before.real:
                            down(before, c + FC - DOWN_LAG)
                    elif t.real:
                        down(t, c - DOWN_LAG)
                    if c == 1 and behind.real:
                        rows_to_features(behind)
                if before.real:
                    features_to_rows(before)

            tile_pipeline(pe, tile_step, 1)

        @block.scalar
        def _(act):
            act.wait_ge(s["ones_set"], 1)
            nc.scalar.activation(table_load[:], ones_row[0:1, 0:1], ACT.Exp)
            act.wait_ge(s["consts_set"], 2)

            def split_high(e):
                after(act, f"wraw_in{e % 2}", (e // 2 + 1) * 16)
                nc.scalar.copy(wres[:, e, 0, :], wraw[e % 2][:]).then_inc(s["w_high"], 1)

            def apply(dst, src, at, o, done):
                for j in range(SUB):
                    last = nc.scalar.activation(dst[:, j, 0:D], src[:, j, :], ACT.Identity, bias=nb[o][:, at + j:at + j + 1],
                                                scale=rs[o][:, at + j:at + j + 1])
                last.then_inc(s[done], 1)

            def step(i, par):
                b, c, e, o = i, i - 1, i - 3, 1 - par
                if on(i, 1):
                    after(act, "vs_psum", c + 1)
                    after(act, "num_psum", c)
                    nc.scalar.copy(vrow[0:1, 0:D], kvp[0:1, 0:D]).then_inc(s["v_row"], 1)
                if on(i, 3):
                    after(act, "nb_ready", i + 2, alone=True)
                    if shares_rows(e):
                        after(act, f"scat{o}", (e - o) * (SUB * TOP_K * 8), alone=True)
                    apply(rows_of(e, o), x2[o], SUB, o, "yn_ready")
                if on(i, 3):
                    after(act, "y_tr", e + 1)
                    after(act, "gate_psum", e)
                    nc.scalar.copy(yT[:], XB[:]).then_inc(s["yT_ready"], 1)
                if on(i, -1):
                    after(act, "nb_ready", i + 2, alone=True)
                    after(act, "xnT_psum", i + 1)
                    apply(xn, xin[o], 0, o, "xn_ready")
                if on(i, 3):
                    after(act, "gate_psum", e + 1)
                    after(act, "lg_sub", e)
                    nc.scalar.copy(lgs[:], XB[:, 0:SUB * E].rearrange("p (j e) -> p j e", j=SUB)).then_inc(s["lgs_ready"], 1)
                if on(i, 3):
                    after(act, "lg_sub", i - 2)
                    nc.scalar.activation(ex[:], lg[:], ACT.Exp).then_inc(s["ex_ready"], 1)
                if on(i, 0):
                    after(act, "k_sin", b + 1)
                    after(act, "kv_psum", b)
                    nc.scalar.copy(vtok[:, :, 0:D], kvp[:].rearrange("p (j c) -> p j c", j=SUB)[:, :, D:2 * D]
                                   ).then_inc(s["vtok_ready"], 1)
                if on(i, -1):
                    after(act, "xnT_psum", i + 2)
                    after(act, "conv_psum", i)
                    after(act, "vs_psum", i)
                    nc.scalar.activation(xnT_h[o][:, PAD:PAD + S], XB[:], ACT.Copy, accum_out=xsum[o][:]).then_inc(s["xnTh_ready"], 1)
                if on(i, 0):
                    after(act, "g_psum", b + 1)
                    after(act, "o_ready", b - 1)
                    nc.scalar.copy(gT[par][:], GW[:]).then_inc(s["g_saved"], 1)
                if isinstance(i, int) and 0 <= i < E // 2:
                    split_high(2 * i)
                    split_high(2 * i + 1)

            pipeline(act, step)
            nc.scalar.activation(table_load[:], ones_row[0:1, 0:1], ACT.Silu)

            def x_high(t):
                after(act, "x_tr", t.no + 1)
                after(act, "h_psum", (t.no - 2) * FC)
                nc.scalar.copy(xT_h[t.buf][:], XB[:]).then_inc(s["xTh_ready"], 1)

            def tile_step(t):
                before, behind = t.at(-1), t.at(1)
                for c in range(FC):
                    if t.real:
                        n = t.no * FC + c
                        if c == 0:
                            after(act, f"bst_in{t.buf}", t.fills * 16, alone=True)
                        after(act, "h_psum", n + 1, alone=True)
                        after(act, "h_low", n - FC + 1)
                        nc.scalar.activation(hf[c][:], hbank(t, c)[:], ACT.Silu, bias=bst[t.buf][:, c:c + 1]).then_inc(s["h_silu"], 1)
                    if c == 1 and behind.real:
                        x_high(behind)
                    if c == DOWN_LAG and before.real:
                        after(act, "y_psum", before.no + 1, alone=True)
                        after(act, "yo_tr", before.no)
                        nc.scalar.activation(yTs[:], YB[before.buf][:], ACT.Identity,
                                             bias=bst[before.buf][:, FC:FC + 1]).then_inc(s["yT_saved"], 1)

            x_high(Tile(0, 0))
            tile_pipeline(act, tile_step, 1)

        @block.gpsimd
        def _(pool):
            nc.gpsimd.memset(half[:], -0.5).then_inc(s["consts_set"], 1)
            nc.gpsimd.memset(ones_row[:], 1.0)
            nc.gpsimd.memset(one16[:], 1.0)
            nc.gpsimd.memset(vtok[:, :, D:D + 1], 1.0)
            nc.gpsimd.memset(vrow[0:1, D:ND], float(S)).then_inc(s["ones_set"], 1)
            pool.wait_ge(s["consts_set"], 1)

            def to_experts(f, o, k):
                if k == 0:
                    after(pool, "yn_ready", f + 1, alone=True)
                    after(pool, "w_kept", f + 1, alone=True)
                    after(pool, "id_kept", f + 1, alone=True)
                    after(pool, "slots_ready", f + 1, alone=True)
                for j in range(SUB):
                    nc.gpsimd.indirect_dma_start(
                        rows_in, bass.IndirectOffsetOnAxis(ap=slots[o][:, k, j:j + 1], axis=0),
                        rows_of(f, o)[:, j, :], None).then_inc(s[f"scat{o}"], 16)

            def step(i, par):
                b, f = i, i - 4
                if on(i, 0):
                    after(pool, "q_sin", b + 1)
                    after(pool, "num_psum", b - 1)
                    nc.gpsimd.tensor_tensor(qrot[par][:], q_c[:], q_s[:], ALU.add).then_inc(s["q_rot"], 1)
                if on(i, 4):
                    to_experts(f, par, 0)
                if on(i, 0):
                    after(pool, "k_sin", b + 1)
                    after(pool, "kv_psum", b)
                    nc.gpsimd.tensor_tensor(ktok[:], k_c[:], k_s[:], ALU.add).then_inc(s["ktok_ready"], 1)
                    if on(i, 4):
                        to_experts(f, par, 1)
                if has_ln(i):
                    after(pool, "ve_ready", i + 3)
                    after(pool, "xn_ready", all_of(i + 1))
                    after(pool, "yn_ready", i - 3)
                    nc.gpsimd.tensor_tensor(rs[par][:], ve[:], half[:], ALU.pow).then_inc(s["ln_rs"], 1)
                if on(i, 4) and not on(i, 0):
                    to_experts(f, par, 1)

            pipeline(pool, step)

            pool.wait_ge(s["x2_out0"], NB // 2 * 16)
            pool.wait_ge(s["x2_out1"], NB // 2 * 16)
            pool.wait_ge(s["out_dummy"], 16)

            def tile_step(t):
                after(pool, "yo_ready", t.no + 1, alone=True)
                after(pool, "acc_done", t.no * (TSUB * 16), alone=True)
                for j in range(TSUB):
                    nc.gpsimd.indirect_dma_start(
                        out, bass.IndirectOffsetOnAxis(ap=tok[t.buf][:, j:j + 1], axis=0),
                        yo[t.buf][:, j, :], None, compute_op=ALU.add).then_inc(s["acc_done"], 16)

            tile_pipeline(pool, tile_step, 0)

        @block.vector
        def _(dve):
            for i in range(2):
                nc.vector.memset(xnT_h[i][:].bitcast(F32), 0.0)
                nc.vector.memset(xnT_l[i][:].bitcast(F32), 0.0)
            for i in range(2):
                nc.vector.memset(mv[i][:], 0.0)
            nc.vector.memset(macc[:], 0.0)
            nc.vector.memset(macc16[:], 0.0).then_inc(s["consts_set"], 1)
            dve.wait_ge(s["consts_set"], 2)

            def statistic(i, par, n):
                second, j = n // SUB % 2 == 0, n % SUB
                at = SUB + j if second else j
                if not on(i, 2 if second else -2):
                    return
                count = i - 1 if second else i + 3
                st_sem, mv_sem = ("st2_ready", "mv2_ready") if second else ("st1_ready", "mv1_ready")
                if n < 2 * SUB:
                    if j == 0:
                        after(dve, mv_sem, count - 1, alone=True)
                        if second:
                            after(dve, "x2_ready", count, alone=True)
                        else:
                            after(dve, f"xin_full{par}", (i + 2 - par) * 8 + 16, alone=True)
                    last = nc.vector.bn_stats(st[:, at, :], (x2 if second else xin)[par][:, j, :])
                    if j == SUB - 1:
                        last.then_inc(s[st_sem], 1)
                else:
                    if j == 0:
                        after(dve, st_sem, count, alone=True)
                        after(dve, "nb_ready", i + 1, alone=True)
                    last = nc.vector.bn_aggr(mv[par][:, at, :], st[:, at, :])
                    if j == SUB - 1:
                        last.then_inc(s[mv_sem], 1)

            def variances(i, par):
                after(dve, "mv1_ready", min(i + 3, NB) if isinstance(i, int) else i + 3)
                after(dve, "mv2_ready", i - 1)
                after(dve, "ln_rs", i + 2)
                nc.vector.tensor_scalar(ve[:], mv[par][:, :, 1], EPS, None, ALU.add).then_inc(s["ve_ready"], 1)

            def low_tokens(i, o):
                if on(i, -1):
                    after(dve, "xnTh_ready", i + 2)
                    after(dve, "conv_psum", i)
                    nc.vector.tensor_tensor(xnT_l[o][:, PAD:PAD + S], XB[:], xnT_h[o][:, PAD:PAD + S].bitcast(F32),
                                            ALU.subtract).then_inc(s["xnTl_ready"], 1)

            def bc(ap):
                return ap[:].unsqueeze(2).to_broadcast([P, SUB, E])

            def chain(n, i=NB, par=0):
                done = [n]

                def link(ins, between=None):
                    done[0] = done[0] + 1
                    ins.then_inc(s["rt"], 1)
                    if between is not None and not (isinstance(i, int) and i >= NB):
                        statistic(i, par, between)
                    after(dve, "rt", done[0])
                return link

            def shift_logits(b):
                link = chain(b * RT_STEPS)
                after(dve, "lgs_ready", b + 1)
                link(nc.vector.tensor_reduce(red[:], lgs[:], AX_X, ALU.max))
                after(dve, "ex_ready", b)
                nc.vector.tensor_tensor(lg[:], lgs[:], bc(red), ALU.subtract).then_inc(s["lg_sub"], 1)

            def choose(i, par):
                b = i - 3
                link = chain(b * RT_STEPS + 1, i, par)
                after(dve, "ex_ready", b + 1)
                link(nc.vector.tensor_reduce(red[:], ex[:], AX_X, ALU.add), 4)
                link(nc.vector.reciprocal(red[:], red[:]), 5)
                link(nc.vector.tensor_tensor(pr[:], ex[:], bc(red), ALU.mult), 6)

                def pick(src, hot, n):
                    n = [n + k if n + k < 4 * SUB else None for k in range(5)]
                    link(nc.vector.tensor_reduce(red[:], src[:], AX_X, ALU.max), n[0])
                    link(nc.vector.tensor_tensor(hot, src[:], bc(red), ALU.is_equal), n[1])
                    link(nc.vector.tensor_tensor(tmp8[:], hot, rankw, ALU.mult), n[2])
                    link(nc.vector.tensor_reduce(red[:], tmp8[:], AX_X, ALU.max), n[3])
                    link(nc.vector.tensor_tensor(hot, tmp8[:], bc(red), ALU.is_equal), n[4])

                pick(pr, oh[:, 0], 7)
                low_tokens(i, 1 - par)
                link(nc.vector.scalar_tensor_tensor(pr2[:], oh[:, 0], -2.0, pr[:], ALU.mult, ALU.add), 12)
                pick(pr2, oh[:, 1], 13)
                link(nc.vector.tensor_tensor(ohs[:], oh[:, 0], oh[:, 1], ALU.add))
                if has_ln(i) and not (isinstance(i, int) and i >= NB):
                    variances(i, par)
                after(dve, "rank_psum", b)
                nc.vector.tensor_copy(oh16[:], ohs[:]).then_inc(s["oh_ready"], 1)
                rows = rows_of(b, 1 - par)
                if shares_rows(b):
                    after(dve, f"scat{1 - par}", (b - 1 + par) * (SUB * TOP_K * 8), alone=True)
                nc.vector.tensor_tensor(rows[:, :, W_AT:W_AT + E], ohs[:], pr[:], ALU.mult).then_inc(s["w_kept"], 1)
                nc.vector.tensor_copy(rows[:, :, ID_AT], ids[:, subtiles(b)]).then_inc(s["id_kept"], 1)
                link(nc.vector.tensor_reduce(msum[:], ohs[:].rearrange("p j e -> p e j"), AX_X, ALU.add))
                link(nc.vector.tensor_tensor(macc[:], macc[:], msum[:], ALU.add))

            def place(b, par):
                link = chain(b * RT_STEPS + 18)
                after(dve, "rank_psum", b + 1)
                ranks = XB[:, 0:SUB * E].rearrange("p (j e) -> p j e", j=SUB)
                nc.vector.tensor_tensor(rk[:], ranks, reg0, ALU.add).then_inc(s["rk_read"], 1)
                link(nc.vector.tensor_copy(macc16[:], macc[:]))
                after(dve, "rk_read", b + 1)
                link(nc.vector.tensor_tensor(tmp16[:], oh[:], rk[:].unsqueeze(1).to_broadcast([P, TOP_K, SUB, E]), ALU.mult))
                link(nc.vector.tensor_reduce(slot_f[:], tmp16[:], AX_X, ALU.add))
                if not isinstance(b, int) or b > 1:
                    after(dve, f"scat{par}", (b - par) * (SUB * TOP_K * 8), alone=True)
                nc.vector.tensor_copy(slots[par][:], slot_f[:]).then_inc(s["slots_ready"], 1)

            def split_low(e):
                after(dve, "w_high", e + 1)
                nc.vector.tensor_tensor(wres[:, e, 1, :], wraw[e % 2][:], wres[:, e, 0, :].bitcast(F32),
                                        ALU.subtract).then_inc(s["w_low"], 1)

            def split_projections():
                dve.wait_ge(s["first_in"], 16)
                nc.vector.tensor_copy(wproj_h[:], wproj).then_inc(s["wsplit"], 1)
                dve.wait_ge(s["wsplit"], 1)
                nc.vector.tensor_tensor(wproj_l[:], wproj, wproj_h[:].bitcast(F32), ALU.subtract).then_inc(s["wsplit"], 1)

            def split_convolution():
                dve.wait_ge(s["second_in"], 16)
                nc.vector.tensor_tensor(wconv[:], lrows, wproj[:, 4:5, :].to_broadcast([P, TAPS, D]),
                                        ALU.mult).then_inc(s["wsplit"], 1)
                nc.vector.tensor_copy(bef16[:], bef).then_inc(s["bef_set"], 1)
                dve.wait_ge(s["wsplit"], 3)
                nc.vector.tensor_copy(wconv_h[:], wconv[:]).then_inc(s["wsplit"], 1)
                dve.wait_ge(s["wsplit"], 4)
                nc.vector.tensor_tensor(wconv_l[:], wconv[:], wconv_h[:].bitcast(F32), ALU.subtract).then_inc(s["wsplit"], 1)
                dve.wait_ge(s["tabk_in"], 16)

            def step(i, par):
                b, c, d, o = i, i - 1, i - 2, 1 - par
                if isinstance(i, int) and i == -1:
                    split_projections()
                if isinstance(i, int) and i == 0:
                    split_convolution()
                if on(i, 1):
                    after(dve, "kv_psum", c + 1)
                    after(dve, "num_psum", c)
                    nc.vector.tensor_tensor(kvbd[:, 0:D], KV[:, 0:D], hmask[:, 0:D], ALU.mult)
                    nc.vector.tensor_scalar(kvbd[:, D:ND], hmask[:, D:ND], KV[:, D:D + 1], None,
                                            ALU.mult).then_inc(s["ks_masked"], 1)
                if on(i, 0):
                    after(dve, "q_psum", b + 1)
                    after(dve, "q_rot", b)
                    nc.vector.tensor_tensor(q_c[:], qp[:, 0:512], cosT, ALU.mult)
                    after(dve, "qp_psum", b + 1)
                    nc.vector.tensor_tensor(q_s[:], qp[:, 512:1024], sinT, ALU.mult).then_inc(s["q_sin"], 1)
                if has_ln(i - 1):
                    after(dve, "ln_rs", i + 2)
                    after(dve, "xn_ready", all_of(i))
                    after(dve, "yn_ready", i - 4)
                    nc.vector.scalar_tensor_tensor(nb[o][:], mv[o][:, :, 0], -1.0, rs[o][:], ALU.mult,
                                                   ALU.mult).then_inc(s["nb_ready"], 1)
                if on(i, 4):
                    place(i - 4, par)
                if on(i, 2):
                    after(dve, "wo_psum", d + 1)
                    after(dve, f"xre_full{par}", (d - par) * 8 + 16)
                    after(dve, "yn_ready", d - 1)
                    if not isinstance(i, int) or d > 1:
                        after(dve, f"x2_out{par}", (d - par) * 8)
                    nc.vector.tensor_tensor(x2[par][:], GW[:].rearrange("p (j d) -> p j d", j=SUB), xre[par][:],
                                            ALU.add).then_inc(s["x2_ready"], 1)
                if on(i, 1):
                    after(dve, "num_psum", c + 1)
                    v = qp[:].rearrange("p (n m) -> p n m", n=2)[:, :, 0:2 * ND].rearrange("p n (j m) -> p n j m", j=2)
                    nc.vector.reciprocal(rden[:].rearrange("p (n j) h -> p n j h", n=2), v[:, :, :, D:ND]
                                         ).then_inc(s["rden_ready"], 1)
                    after(dve, "rden_ready", c + 1)
                    after(dve, "a_tr", c)
                    for n in range(2):
                        last = nc.vector.tensor_tensor(
                            att[:, 2 * n:2 * n + 2, :].rearrange("p j (h e) -> p j h e", h=H),
                            v[:, n, :, 0:D].rearrange("p j (h e) -> p j h e", h=H),
                            rden[:, 2 * n:2 * n + 2, :].unsqueeze(3).to_broadcast([P, 2, H, DK]), ALU.mult)
                    last.then_inc(s["att_ready"], 1)
                hurry = isinstance(i, int) and i >= NB
                for n in range(4 * SUB if hurry else SUB):
                    statistic(i, par, n)
                if hurry and has_ln(i):
                    variances(i, par)
                if on(i, 0):
                    after(dve, "kvp_psum", b + 1)
                    after(dve, "ktok_ready", b)
                    k = kvp[:].rearrange("p (j c) -> p j c", j=SUB)[:, :, 0:D]
                    nc.vector.tensor_tensor(k_c[:], k, tabk[:, 0], ALU.mult)

                    def halves(v, t):
                        return v.rearrange("p j (h t e) -> p j h t e", h=H, t=2)[:, :, :, t, :]
                    for t in range(2):
                        last_k = nc.vector.tensor_tensor(halves(k_s[:], t), halves(k, 1 - t), halves(tabk[:, 1], t), ALU.mult)
                    last_k.then_inc(s["k_sin"], 1)
                if on(i, 3):
                    shift_logits(i - 3)
                if on(i, 1):
                    after(dve, "a_tr", c + 1)
                    after(dve, "wo_psum", c)
                    nc.vector.scalar_tensor_tensor(oT[:], CV[:], lb, gT[o][:], ALU.add,
                                                   ALU.mult).then_inc(s["o_ready"], 1)
                if on(i, 3):
                    choose(i, par)
                else:
                    for n in range(SUB, 4 * SUB):
                        statistic(i, par, n)
                    low_tokens(i, o)
                    if has_ln(i) and not hurry:
                        variances(i, par)
                if isinstance(i, int) and 0 <= i < E // 2:
                    split_low(2 * i)
                    split_low(2 * i + 1)

            pipeline(dve, step)

            tb = [0]

            def link(ins):
                tb[0] += 1
                ins.then_inc(s["tb"], 1)
                dve.wait_ge(s["tb"], tb[0])

            def row(ap, n, m):
                return ap[0:1, :].unsqueeze(1).to_broadcast([1, n, m])

            nk = N_COUNT
            dve.wait_ge(s["cnt_psum"], 1)
            dve.wait_ge(s["rowc_in"], 16)
            link(nc.vector.tensor_copy(cnt[:], GW[0:1, 0:E]))
            nc.vector.tensor_tensor(fill_at[:], cnt[:], reg0[0:1, 0, :], ALU.add).then_inc(s["fill_ready"], 1)
            link(nc.vector.tensor_tensor(gt[:], thr, cnt[:].unsqueeze(2).to_broadcast([1, E, nk]), ALU.is_lt))
            link(nc.vector.tensor_reduce(ntile[:], gt[:], AX_X, ALU.add))
            link(nc.vector.tensor_tensor(cm[:], cumu, row(ntile, E, E), ALU.mult))
            link(nc.vector.tensor_reduce(incl[:], cm[:], AX_X, ALU.add))
            link(nc.vector.tensor_scalar(skip[:], ntile[:], -float(TS), float(CAP), ALU.mult, ALU.add))
            link(nc.vector.tensor_tensor(passed[:], row(incl, N_TILES, E), tno, ALU.is_le))
            link(nc.vector.tensor_tensor(pskip[:], passed[:], row(skip, N_TILES, E), ALU.mult))
            link(nc.vector.tensor_reduce(trow_f[:], pskip[:], AX_X, ALU.add))
            link(nc.vector.scalar_tensor_tensor(trow_f[:], tno[:, :, 0], float(TS), trow_f[:], ALU.mult, ALU.add))
            nc.vector.tensor_scalar(trow[:], trow_f[:], float(E * CAP), None, ALU.min).then_inc(s["table_ready"], 1)
            link(nc.vector.tensor_reduce(texp_f[:], passed[:], AX_X, ALU.add))
            nc.vector.tensor_scalar(texp[:], texp_f[:], float(E - 1), None, ALU.min).then_inc(s["table_ready"], 1)

            def x_low(t):
                after(dve, "xTh_ready", t.no + 1)
                nc.vector.tensor_tensor(xT_l[t.buf][:], XB[:], xT_h[t.buf][:].bitcast(F32),
                                        ALU.subtract).then_inc(s["xTl_ready"], 1)

            def weights(t):
                after(dve, f"bst_in{t.buf}", t.fills * 16)
                after(dve, f"xg_in{t.buf}", t.fills * 16)
                nc.vector.tensor_tensor(wsel[:], xg[t.buf][:, :, W_AT:W_AT + E],
                                        bst[t.buf][:, FC + 1:BPACK].unsqueeze(1).to_broadcast([P, TSUB, E]),
                                        ALU.mult).then_inc(s["wsel_ready"], 1)
                after(dve, "yo_ready", t.no - 2)
                nc.vector.tensor_copy(tok_f[t.buf][:], xg[t.buf][:, :, ID_AT])
                after(dve, "wsel_ready", t.no + 1)
                nc.vector.tensor_reduce(wv[t.buf][:], wsel[:], AX_X, ALU.add).then_inc(s["wv_ready"], 1)

            def weigh(t):
                after(dve, "wv_ready", t.no + 1)
                after(dve, "acc_done", (t.no - 2) * (TSUB * 16))
                nc.vector.tensor_copy(tok[t.buf][:], tok_f[t.buf][:])
                after(dve, "yo_tr", t.no + 1)
                nc.vector.tensor_tensor(yo[t.buf][:], TY[:].rearrange("p (j d) -> p j d", j=TSUB),
                                        wv[t.buf][:].unsqueeze(2).to_broadcast([P, TSUB, D]), ALU.mult).then_inc(s["yo_ready"], 1)

            def tile_step(t):
                before, behind = t.at(-1), t.at(1)
                for c in range(FC):
                    if t.real:
                        n = t.no * FC + c
                        after(dve, "h_silu", n + 1)
                        after(dve, "h_psum", n)
                        nc.vector.tensor_copy(hh[c][:], hf[c][:]).then_inc(s["h_high"], 1)
                        after(dve, "h_high", n + 1)
                        nc.vector.tensor_tensor(hl[c][:], hf[c][:], hh[c][:].bitcast(F32), ALU.subtract).then_inc(s["h_low"], 1)
                    if c == 1 and behind.real:
                        x_low(behind)
                        weights(behind)
                if before.real:
                    weigh(before)

            x_low(Tile(0, 0))
            weights(Tile(0, 0))
            tile_pipeline(dve, tile_step, 1)


RT_STEPS = 21
_INS = ["x", "first", "second", "tables_k", "tail_rows", "row_consts", "w_experts", "b_experts"]


def rope_tables():
    inv = (np.float32(1.0) / np.float32(10000.0) ** (np.arange(0, DK, 2, dtype=np.float32) / np.float32(DK))).astype(np.float32)
    freqs = np.arange(S, dtype=np.float32)[:, None] * inv[None, :]
    emb = np.concatenate([freqs, freqs], axis=1)
    sign = np.where(np.arange(DK) < DK // 2, -1.0, 1.0).astype(np.float32)
    cos = np.tile(np.cos(emb).astype(np.float32), (1, H))
    sin = np.tile(np.sin(emb).astype(np.float32) * sign[None, :], (1, H))
    return cos, sin


def head_masks():
    head = np.arange(D) // DK
    full = (head[:, None] == head[None, :]).astype(np.float32)
    each = (head[:, None] == np.arange(H)[None, :]).astype(np.float32)
    return np.concatenate([full, each], axis=1) * np.float32(DK ** -0.5)


def constants():
    cos, sin = rope_tables()
    f = np.float32
    tail = np.zeros((TS, ROW), f)
    tail[:, ID_AT] = N_TOK + np.arange(TS)
    experts = np.arange(E, dtype=f)
    thresholds = np.broadcast_to(np.arange(0, N_TOK, TS, dtype=f), (E, N_COUNT))
    tile_no = np.broadcast_to(np.arange(N_TILES, dtype=f)[:, None], (N_TILES, E))
    return {
        "cos_t": cos.T, "sin_t": sin.T, "head_mask": head_masks(), "ident": np.eye(P, dtype=f),
        "tables_k": np.stack([cos, sin]).reshape(2, SUB, P, D).transpose(2, 0, 1, 3),
        "rank_w": np.tile(E - experts, (P, SUB)),
        "region": np.tile(experts * CAP, (P, SUB)),
        "before": np.triu(np.ones((P, P), f), 1),
        "ids": np.arange(N_TOK, dtype=f).reshape(NB * SUB, P).T,
        "tail_rows": tail.reshape(P, TSUB, ROW),
        "row_consts": np.concatenate([thresholds.reshape(-1), np.tril(np.ones((E, E), f)).reshape(-1), tile_no.reshape(-1)])[None],
    }


def kernel(**inputs):
    import concourse.bacc as _bacc
    from concourse.bass_utils import run_bass_kernel_spmd as _run

    g = {n: np.asarray(v) for n, v in inputs.items()}
    rot = np.arange(D).reshape(H, 2, DK // 2)[:, ::-1].reshape(-1)
    wq, wk, wv, wg = (g[f"L0_attn_{n}"] for n in ("Wq", "Wk", "Wv", "Wg"))
    w1, w2 = g["L0_ffn_w1"], g["L0_ffn_w2"]
    b1 = g["L0_ffn_b1"].reshape(E, FC, P).transpose(2, 0, 1)
    b2 = g["L0_ffn_b2"].T[:, :, None]
    code = np.broadcast_to(np.eye(E, dtype=b1.dtype), (P, E, E))
    lay = {
        **constants(),
        "x": g["L0_attn_hidden_states"].reshape(N_TOK, D),
        "w_proj": np.concatenate([wq.T, wq[rot].T, wg.T, wk.T, wv.T], axis=1),
        "w_o": g["L0_attn_Wo"].T,
        "lepe_rows": np.broadcast_to(g["L0_attn_lepe_w"].reshape(D, TAPS).T.reshape(-1), (P, TAPS * D)),
        "lepe_b": g["L0_attn_lepe_b"].reshape(D, 1),
        "gate_t": g["L0_ffn_gate_w"].T,
        "w_experts": np.concatenate([w1, w2.reshape(E, FC, P, D).transpose(0, 2, 1, 3).reshape(E, P, FC * D)], axis=2),
        "b_experts": np.concatenate([b1, b2, code], axis=2),
    }
    lay["first"] = np.concatenate([lay[n] for n in FIRST], axis=1)
    lay["second"] = np.concatenate([lay[n] for n in SECOND], axis=1)
    nc = _bacc.Bacc("TRN2", target_bir_lowering=False, num_devices=1)
    arrays, args = {}, []
    for name in _INS:
        a = np.ascontiguousarray(lay[name])
        arrays[f"in_{name}"] = a
        args.append(nc.dram_tensor(f"in_{name}", a.shape, mybir.dt.from_np(a.dtype), kind="ExternalInput").ap())
    args.append(nc.dram_tensor("out_x", (N_TOK + TS, D), F32, kind="ExternalOutput").ap())
    build(nc, *args)
    r = _run(nc, [arrays], core_ids=[0])
    return r.results[0]["out_x"][:N_TOK].reshape(NB, S, D)
```
